# Optimizing a Trainium2 kernel written in Bass

```python
import numpy as np
import jax
import jax.numpy as jnp

def _softmax(x, axis=-1):
    return jax.nn.softmax(x, axis=axis)

def _gelu(x):
    return jax.nn.gelu(x, approximate=True)

def _silu(x):
    return jax.nn.silu(x)

def _sigmoid(x):
    return jax.nn.sigmoid(x)

def _layernorm(x, axis=-1, eps=1e-05):
    m = jnp.mean(x, axis=axis, keepdims=True)
    v = jnp.var(x, axis=axis, keepdims=True)
    return (x - m) / jnp.sqrt(v + eps)

def _scatter_add(tgt, idx, src, axis=0):
    return tgt.at[idx].add(src)

def _segment_sum(src, seg, n):
    return jax.ops.segment_sum(src, seg, n)
kernel_name = 'mk_adaln_d1_jaxref_r8_784c1a'

def setup_inputs(seed: int=0):
    np.random.seed(seed)
    _w = jnp.asarray

    def _L0_attn_setup():
        import jax, jax.numpy as jnp
        import numpy as np
        EMBED_DIM = 128
        NUM_HEADS = 16
        HEAD_DIM = EMBED_DIM // NUM_HEADS
        SCALING = HEAD_DIM ** (-0.5)
        EPS = 1e-05

        def _rope(seq_len):
            inv_freq = 1.0 / 10000.0 ** (jnp.arange(0, HEAD_DIM, 2, dtype=jnp.float32) / HEAD_DIM)
            freqs = jnp.arange(seq_len, dtype=jnp.float32)[:, None] * inv_freq[None, :]
            emb = jnp.concatenate([freqs, freqs], axis=-1)
            return (jnp.cos(emb), jnp.sin(emb))

        def _rotate(x, cos, sin):
            d = x.shape[-1]
            x1, x2 = (x[..., :d // 2], x[..., d // 2:])
            rotated = jnp.concatenate([-x2, x1], axis=-1)
            return x * cos + rotated * sin
        key = jax.random.key(seed)
        ks = jax.random.split(key, 6)
        B, S, D = (2, 256, EMBED_DIM)
        scale = D ** (-0.5)
        return {'x': jax.random.normal(ks[0], (B, S, D), jnp.float32), 'Wq': jax.random.normal(ks[1], (D, D), jnp.float32) * scale, 'Wk': jax.random.normal(ks[2], (D, D), jnp.float32) * scale, 'Wv': jax.random.normal(ks[3], (D, D), jnp.float32) * scale, 'Wg': jax.random.normal(ks[4], (D, D), jnp.float32) * scale, 'Wo': jax.random.normal(ks[5], (D, D), jnp.float32) * scale, 'gn_w': jnp.ones((D,), jnp.float32), 'gn_b': jnp.zeros((D,), jnp.float32)}
    _L0_attn_in = _L0_attn_setup()

    def _L0_ffn_setup():
        import jax, jax.numpy as jnp
        import numpy as np
        DIM = 128
        HID = 256
        OUT = 128
        NE = 8
        TOPK = 2

        def _xavier(key, shape):
            fan_in, fan_out = (shape[-2], shape[-1])
            lim = jnp.sqrt(6.0 / (fan_in + fan_out))
            return jax.random.uniform(key, shape, jnp.float32, -lim, lim)
        key = jax.random.key(seed)
        ks = jax.random.split(key, 8)
        X = jax.random.normal(ks[0], (4, 128, DIM), jnp.float32)
        W1 = _xavier(ks[1], (NE, DIM, HID))
        W3 = _xavier(ks[2], (NE, DIM, HID))
        W2 = _xavier(ks[3], (NE, HID, OUT))
        b1 = jnp.zeros((NE, HID), jnp.float32)
        b3 = jnp.zeros((NE, HID), jnp.float32)
        b2 = jnp.zeros((NE, OUT), jnp.float32)
        Wg = _xavier(ks[4], (DIM, NE))
        bg = jnp.zeros((NE,), jnp.float32)
        Wf = _xavier(ks[5], (OUT, OUT))
        bf = jnp.zeros((OUT,), jnp.float32)
        return {'X': X, 'W1': W1, 'b1': b1, 'W3': W3, 'b3': b3, 'W2': W2, 'b2': b2, 'Wg': Wg, 'bg': bg, 'Wf': Wf, 'bf': bf}
    _L0_ffn_in = _L0_ffn_setup()
    _L0_c = _w((lambda *s: np.random.randn(*s).astype(np.float32) * 0.05)(4, 128))
    _L0_wmod = _w((lambda *s: np.random.randn(*s).astype(np.float32) * 0.05)(128, 6 * 128) * 128 ** (-0.5))
    _d = {'L0_attn_x': _L0_attn_in['x'], 'L0_attn_Wq': _L0_attn_in['Wq'], 'L0_attn_Wk': _L0_attn_in['Wk'], 'L0_attn_Wv': _L0_attn_in['Wv'], 'L0_attn_Wg': _L0_attn_in['Wg'], 'L0_attn_Wo': _L0_attn_in['Wo'], 'L0_attn_gn_w': _L0_attn_in['gn_w'], 'L0_attn_gn_b': _L0_attn_in['gn_b'], 'L0_ffn_W1': _L0_ffn_in['W1'], 'L0_ffn_b1': _L0_ffn_in['b1'], 'L0_ffn_W3': _L0_ffn_in['W3'], 'L0_ffn_b3': _L0_ffn_in['b3'], 'L0_ffn_W2': _L0_ffn_in['W2'], 'L0_ffn_b2': _L0_ffn_in['b2'], 'L0_ffn_Wg': _L0_ffn_in['Wg'], 'L0_ffn_bg': _L0_ffn_in['bg'], 'L0_ffn_Wf': _L0_ffn_in['Wf'], 'L0_ffn_bf': _L0_ffn_in['bf'], 'L0_c': _L0_c, 'L0_wmod': _L0_wmod}
    _x0 = _d['L0_attn_x']
    _d['L0_attn_x'] = jax.random.normal(jax.random.fold_in(jax.random.key(seed), 1), (4, 512, 128), dtype=_x0.dtype)
    del _x0
    return _d

def reference(L0_attn_x, L0_attn_Wq, L0_attn_Wk, L0_attn_Wv, L0_attn_Wg, L0_attn_Wo, L0_attn_gn_w, L0_attn_gn_b, L0_ffn_W1, L0_ffn_b1, L0_ffn_W3, L0_ffn_b3, L0_ffn_W2, L0_ffn_b2, L0_ffn_Wg, L0_ffn_bg, L0_ffn_Wf, L0_ffn_bf, L0_c, L0_wmod):

    def _L0_attn_ref(x, Wq, Wk, Wv, Wg, Wo, gn_w, gn_b):
        import jax, jax.numpy as jnp
        import numpy as np
        EMBED_DIM = 128
        NUM_HEADS = 16
        HEAD_DIM = EMBED_DIM // NUM_HEADS
        SCALING = HEAD_DIM ** (-0.5)
        EPS = 1e-05

        def _rope(seq_len):
            inv_freq = 1.0 / 10000.0 ** (jnp.arange(0, HEAD_DIM, 2, dtype=jnp.float32) / HEAD_DIM)
            freqs = jnp.arange(seq_len, dtype=jnp.float32)[:, None] * inv_freq[None, :]
            emb = jnp.concatenate([freqs, freqs], axis=-1)
            return (jnp.cos(emb), jnp.sin(emb))

        def _rotate(x, cos, sin):
            d = x.shape[-1]
            x1, x2 = (x[..., :d // 2], x[..., d // 2:])
            rotated = jnp.concatenate([-x2, x1], axis=-1)
            return x * cos + rotated * sin
        B, S, D = x.shape
        H, Dh = (NUM_HEADS, HEAD_DIM)

        def split_heads(t):
            return t.reshape(B, S, H, Dh).transpose(0, 2, 1, 3)
        q = split_heads(x @ Wq.T)
        k = split_heads(x @ Wk.T)
        v = split_heads(x @ Wv.T)
        cos, sin = _rope(S)
        q = _rotate(q, cos, sin)
        k = _rotate(k, cos, sin)
        retention = jnp.einsum('bhsd,bhtd->bhst', q, k) * SCALING
        gammas = 1.0 - 2.0 ** (-5.0 - jnp.arange(H, dtype=jnp.float32))
        diff = jnp.arange(S)[:, None] - jnp.arange(S)[None, :]
        causal = diff >= 0
        decay = jnp.where(causal, gammas[:, None, None] ** jnp.maximum(diff, 0).astype(jnp.float32), 0.0)
        retention = retention * decay[None]
        out = jnp.einsum('bhst,bhtd->bhsd', retention, v)
        out = out.transpose(0, 2, 1, 3).reshape(B * S, H, Dh)
        mean = out.mean(axis=-1, keepdims=True)
        var = out.var(axis=-1, keepdims=True)
        out = (out - mean) * jax.lax.rsqrt(var + EPS)
        out = out * gn_w.reshape(H, Dh) + gn_b.reshape(H, Dh)
        out = out.reshape(B, S, D)
        gate = jax.nn.silu(x @ Wg.T)
        return gate * out @ Wo.T

    def _L0_ffn_ref(X, W1, b1, W3, b3, W2, b2, Wg, bg, Wf, bf):
        import jax, jax.numpy as jnp
        import numpy as np
        DIM = 128
        HID = 256
        OUT = 128
        NE = 8
        TOPK = 2

        def _xavier(key, shape):
            fan_in, fan_out = (shape[-2], shape[-1])
            lim = jnp.sqrt(6.0 / (fan_in + fan_out))
            return jax.random.uniform(key, shape, jnp.float32, -lim, lim)
        gating = jax.nn.softmax(X @ Wg + bg, axis=-1)
        top_k_indices = jnp.argsort(gating, axis=-1)[..., -TOPK:]
        h1 = jnp.einsum('bsd,edh->bseh', X, W1) + b1
        h3 = jnp.einsum('bsd,edh->bseh', X, W3) + b3
        h = jax.nn.silu(h1 * h3)
        expert_outputs = jnp.einsum('bseh,eho->bseo', h, W2) + b2
        topk_out = jnp.take_along_axis(expert_outputs, top_k_indices[..., None], axis=2)
        topk_w = jnp.take_along_axis(gating, top_k_indices, axis=-1)
        mixed = jnp.sum(topk_w[..., None] * topk_out, axis=2)
        return mixed @ Wf + bf
    x = L0_attn_x
    mod = (_silu(L0_c) @ L0_wmod).reshape(L0_c.shape[0], 6, 1, -1)
    sa, ca, ga, sb, cb, gb = (mod[:, 0], mod[:, 1], mod[:, 2], mod[:, 3], mod[:, 4], mod[:, 5])
    ga = (2 * (ga >= 0) - 1) * jnp.maximum(jnp.abs(ga), 0.25)
    gb = (2 * (gb >= 0) - 1) * jnp.maximum(jnp.abs(gb), 0.25)
    h = _layernorm(x, axis=-1) * (1 + ca) + sa
    x = x + ga * _L0_attn_ref(h, L0_attn_Wq, L0_attn_Wk, L0_attn_Wv, L0_attn_Wg, L0_attn_Wo, L0_attn_gn_w, L0_attn_gn_b)
    h = _layernorm(x, axis=-1) * (1 + cb) + sb
    x = x + gb * _L0_ffn_ref(h, L0_ffn_W1, L0_ffn_b1, L0_ffn_W3, L0_ffn_b3, L0_ffn_W2, L0_ffn_b2, L0_ffn_Wg, L0_ffn_bg, L0_ffn_Wf, L0_ffn_bf)
    return x

_drawn_inputs = setup_inputs


def setup_inputs(seed=0):
    import zlib

    import numpy as np

    out = dict(_drawn_inputs(seed))
    spreads = {'L0_attn_gn_w': (1.0, 0.2),
     'L0_attn_gn_b': (0.0, 0.537),
     'L0_ffn_b1': (0.0, 0.8),
     'L0_ffn_b3': (0.0, 0.8),
     'L0_ffn_b2': (0.0, 0.634),
     'L0_ffn_bg': (0.0, 0.8),
     'L0_ffn_bf': (0.0, 0.298)}
    factors = {}
    for name, (base, spread) in spreads.items():
        noise = np.random.default_rng([zlib.crc32(name.encode()), seed]).standard_normal(out[name].shape)
        drawn = base * np.exp(spread * noise) if base else spread * noise
        out[name] = jnp.asarray(drawn.astype(out[name].dtype))
    for name, factor in factors.items():
        out[name] = (out[name] * factor).astype(out[name].dtype)
    return out
```

```python
from contextlib import ExitStack

import numpy as np

import concourse.bass as bass
from concourse import mybir

F32 = mybir.dt.float32
F32R = mybir.dt.float32r
ALU = mybir.AluOpType
ACT = mybir.ActivationFunctionType
AX = mybir.AxisListType

P = 128
NB = 4
S = 512
C = S // P
D = 128
H = 16
DH = D // H
NE = 8
HID = 256
KB = HID // P
EPS = 1e-5
TOPK = 2
U = NE * KB
WK, WKR, WQ, WQR, WG, WV = range(6)
SA, CA, SB, CB = range(4)
GA, GB = range(2)


def shape_constants():
    inv_freq = (np.float32(1.0) / np.float32(10000.0) ** (np.arange(0, DH, 2, dtype=np.float32) / np.float32(DH))).astype(np.float32)
    freqs = np.arange(S, dtype=np.float32)[:, None] * inv_freq[None, :]
    emb = np.concatenate([freqs, freqs], axis=-1).astype(np.float64)
    sign = np.where(np.arange(DH) < DH // 2, -1.0, 1.0)
    cos = np.tile(np.cos(emb).T, (H, 1)).astype(np.float32)
    sin = np.tile((np.sin(emb) * sign).T, (H, 1)).astype(np.float32)
    gamma = np.repeat(1.0 - 2.0 ** (-5.0 - np.arange(H)), DH)[:, None].astype(np.float32)
    scale = DH ** -0.5
    row_head, row_dim = np.divmod(np.arange(D), DH)
    gather = np.zeros((D, DH, D))
    for dv in range(DH):
        same = row_head[:, None] == row_head[None, :]
        gather[:, dv, :] = same * ((row_dim[None, :] == dv) - 1.0 / DH) * scale
    mean = (row_head[:, None] == np.arange(H)[None, :]) / DH
    ident = np.eye(P)
    later = np.tile((np.arange(NE)[None, :] > np.arange(NE)[:, None]).reshape(1, -1), (P, 1))
    parts = [cos, sin, gather.reshape(D, -1), ident, mean, gamma, later]
    return np.ascontiguousarray(np.concatenate(parts, axis=1), dtype=np.float32)


CONST_WIDTHS = [S, S, DH * D, P, H, 1, NE * NE]
CONST_AT = [sum(CONST_WIDTHS[:i]) for i in range(len(CONST_WIDTHS) + 1)]


def build(nc, x, w_att, wo_t, gn, w1, b1_t, w3, b3_t, w2, b2, wg, bg, wf, bf, c_t, wmod, consts, out):
    with ExitStack() as ctx:
        def sb(name, *shape, dt=F32):
            return ctx.enter_context(nc.sbuf_tensor(name, [P, *shape], dt))

        def sem(name):
            return ctx.enter_context(nc.semaphore(name))

        cst = sb("cst", CONST_AT[-1])
        cos, sin, gather, ident, mean16, gamma, later = [cst[:, a:b] for a, b in zip(CONST_AT, CONST_AT[1:])]
        gather = gather.rearrange("p (v d) -> p v d", v=DH)
        later = later.rearrange("p (i j) -> p i j", i=NE)
        wat = sb("wat", 6, D)
        wat_hi = sb("wat_hi", 6, D, dt=F32R)
        wat_lo = sb("wat_lo", 6, D, dt=F32R)
        wv_hi = sb("wv_hi", DH, H, DH, dt=F32R)
        wv_lo = sb("wv_lo", DH, H, DH, dt=F32R)
        wo_sb = sb("wo_sb", D)
        gn_sb = sb("gn_sb", 2)
        w13 = sb("w13", 2, NE, HID)
        w13_hi = sb("w13_hi", 2, NE, HID, dt=F32R)
        w13_lo = sb("w13_lo", 2, NE, HID, dt=F32R)
        b13 = sb("b13", 2, U)
        w2_sb = sb("w2_sb", U, D)
        b2_sb = sb("b2_sb", D)
        wg_sb = sb("wg_sb", NE)
        bg_bc = sb("bg_bc", NE)
        wf_sb = sb("wf_sb", D)
        bf_bc = sb("bf_bc", D)
        ct_sb = sb("ct_sb", NB)
        wmod_sb = sb("wmod_sb", 6, D)
        sct = sb("sct", NB)
        sc_bc = sb("sc_bc", NB, P)
        mod = sb("mod", 4, NB)
        gmod = sb("gmod", 2, NB, D)
        gb_bf = sb("gb_bf", NB, D)
        eps = sb("eps", 1)
        xs = sb("xs", NB, C, D)
        stats = sb("stats", 2, 2, C, 6)
        mv = sb("mv", 2, 2, C, 2)
        sd = sb("sd", 2, 2, C)
        rstd = sb("rstd", 2, 2, C)
        xn = sb("xn", 2, C, D)
        h_t = sb("h_t", S)
        h_hi = sb("h_hi", 2, S, dt=F32R)
        h_lo = sb("h_lo", 2, S, dt=F32R)
        rope = sb("rope", 4, S)
        khat = sb("khat", 2, S)
        qhat = sb("qhat", 2, S)
        gate = sb("gate", 2, S)
        kv = sb("kv", 2, S)
        state = sb("state", 3, S)
        qs = sb("qs", 3, S)
        o_sb = sb("o_sb", S)
        o_sq = sb("o_sq", S)
        gsd = sb("gsd", C * H)
        grs = sb("grs", C * H)
        grs_bc = sb("grs_bc", C, D)
        z1 = sb("z1", S)
        z2 = sb("z2", S)
        z3 = sb("z3", S)
        att = sb("att", C, D)
        x2 = sb("x2", 2, C, D)
        x2f = sb("x2f", 2, C, D)
        h2_t = sb("h2_t", S)
        h2_hi = sb("h2_hi", 2, S, dt=F32R)
        h2_lo = sb("h2_lo", 2, S, dt=F32R)
        lg = sb("lg", 3, C, NE)
        lmax = sb("lmax", C)
        lsum = sb("lsum", C)
        lrec = sb("lrec", C)
        prob = sb("prob", 2, C, NE)
        cmp = sb("cmp", 5, C, NE, NE)
        rank = sb("rank", C, NE)
        gw = sb("gw", 2, C, NE)
        gw_t = sb("gw_t", S)
        stage = w13[:].rearrange("p w e h -> p (w e h)").rearrange("p (n s) -> p n s", s=S)
        h1b, hu, hs = stage[:, 0:2], stage[:, 2:4], stage[:, 4:8]
        yg = sb("yg", 2, C, D)
        acc = sb("acc", 2, C, D)
        mix_t = sb("mix_t", S)
        ffg = sb("ffg", C, D)
        g_raw, g_sign, g_abs = acc[:], yg[:], x2f[:]
        ps = ctx.enter_context(nc.psum_tensor("ps", [P, 8, S], F32))
        H1, H3, Y, O, V, M = [ps[:, 0, :], ps[:, 1, :]], [ps[:, 2, :], ps[:, 3, :]], ps[:, 4, :], ps[:, 5, :], ps[:, 6, :], ps[:, 7, :]

        def tiled(ap):
            return ap.rearrange("p (c d) -> p c d", c=C)

        def tile(ap, c):
            return ap[:, c * P:(c + 1) * P]

        def by_head(w):
            return w[:, WV].bitcast(F32).rearrange("p (h v) -> p h v", h=H).unsqueeze(3).to_broadcast([P, H, DH, DH])

        x_in = [sem(f"x_in{b}") for b in range(NB)]
        wat_in, cst_in, mod_in, w13_in, w2_in, small_in = map(sem, ["wat_in", "cst_in", "mod_in", "w13_in", "w2_in", "small_in"])
        eps_set = sem("eps_set")
        sct_ready, scb_ready, mod_ps, mod_ready, gmod_ps, gmod_steps, gbbf_ready = map(sem, [
            "sct_ready", "scb_ready", "mod_ps", "mod_ready", "gmod_ps", "gmod_steps", "gbbf_ready"])
        wv_ready = sem("wv_ready")
        wat_hi_ready, wat_lo_ready, w13_hi_ready, w13_lo_ready = map(sem, ["wat_hi_ready", "wat_lo_ready", "w13_hi_ready", "w13_lo_ready"])
        ln_chain = [sem("ln1_chain"), sem("ln2_chain")]
        sd_ready = [sem("sd1_ready"), sem("sd2_ready")]
        xn_ready = [sem("xn1_ready"), sem("xn2_ready")]
        xt_ps = sem("xt_ps")
        h_ready, h_hi_ready, h_lo_ready = map(sem, ["h_ready", "h_hi_ready", "h_lo_ready"])
        k_ps, q_ps, g_ps, rope_k, rope_q, khat_ready, qhat_ready, gate_ready = map(sem, [
            "k_ps", "q_ps", "g_ps", "rope_k", "rope_q", "khat_ready", "qhat_ready", "gate_ready"])
        v_ps, kv_ready, state_ready, qs_ready, o_step = map(sem, ["v_ps", "kv_ready", "state_ready", "qs_ready", "o_step"])
        osb_ready, osq_ready, var_ps, gsd_ready, grs_ready, grsbc_ready, grst_ps = map(sem, [
            "osb_ready", "osq_ready", "var_ps", "gsd_ready", "grs_ready", "grsbc_ready", "grst_ps"])
        z1_ready, z2_ready, z3_ready, wo_ps, att_ready, x2_ready, x2f_ready = map(sem, [
            "z1_ready", "z2_ready", "z3_ready", "wo_ps", "att_ready", "x2_ready", "x2f_ready"])
        x2t_ps, h2_ready, h2_hi_ready, h2_lo_ready = map(sem, ["x2t_ps", "h2_ready", "h2_hi_ready", "h2_lo_ready"])
        lg_ps, lg_steps, exp_ready, gw_ready, gwt_ps, gwt_ready, b2_ps, acc_set = map(sem, [
            "lg_ps", "lg_steps", "exp_ready", "gw_ready", "gwt_ps", "gwt_ready", "b2_ps", "acc_set"])
        h1_ps, h3_ps, h1b_ready, hu_ready, hs_ready, y_ps, yg_ready, acc_step = map(sem, [
            "h1_ps", "h3_ps", "h1b_ready", "hu_ready", "hs_ready", "y_ps", "yg_ready", "acc_step"])
        mixt_ps, mixt_ready, ff_ps, ffg_ready, res_ready, stored = map(sem, [
            "mixt_ps", "mixt_ready", "ff_ps", "ffg_ready", "res_ready", "stored"])

        LEAD = 3
        SLOTS = range(-U - 2 - LEAD, NB * U + 10)

        def at(g, s):
            b, r = divmod(g - s + U + LEAD, U)
            return b if r == 0 and 0 <= b < NB else None

        LN1, NRM1, HT, PK, PQ, PG, DV0 = -2, -1, 0, 1, 2, 2, 3
        SQ = DV0 + DH + 1
        VAR, RSD, RST, WO, NRM2, LN2, LOG, TOP, GWT, B2 = [SQ + i for i in (1, 2, 3, 4, 5, 6, 7, 8, 9, 10)]
        MIXT, FF = 2 * U + LEAD + 4, 2 * U + LEAD + 5

        SPLIT = HT - U - LEAD

        block = ctx.enter_context(nc.Block())

        @block.sync
        def _(sp):
            sp.dma_start(xs[:, 0], x[0].rearrange("(c p) d -> p c d", p=P)).then_inc(x_in[0], 16)
            sp.dma_start(wat[:], w_att).then_inc(wat_in, 16)
            sp.dma_start(cst[:], consts).then_inc(cst_in, 16)
            for b in range(1, NB):
                sp.dma_start(xs[:, b], x[b].rearrange("(c p) d -> p c d", p=P)).then_inc(x_in[b], 16)
            sp.dma_start(wo_sb[:], wo_t).then_inc(small_in, 16)
            sp.dma_start(gn_sb[:], gn).then_inc(small_in, 16)
            sp.dma_start(wg_sb[:], wg).then_inc(small_in, 16)
            sp.dma_start(bg_bc[:], bg.to_broadcast([P, NE])).then_inc(small_in, 16)
            sp.dma_start(b2_sb[0:NE, :], b2).then_inc(small_in, 16)
            sp.dma_start(wf_sb[:], wf).then_inc(small_in, 16)
            sp.dma_start(bf_bc[:], bf.to_broadcast([P, D])).then_inc(small_in, 16)
            sp.dma_start(b13[:, 0], b1_t).then_inc(small_in, 16)
            sp.dma_start(b13[:, 1], b3_t).then_inc(small_in, 16)
            for b in range(NB):
                sp.wait_ge(res_ready, b + 1)
                sp.dma_start(out[b].rearrange("(c p) d -> p c d", p=P), x2f[:, b % 2]).then_inc(stored, 16)
            sp.wait_ge(stored, 16 * NB)

        SMALL = 9 * 16
        LG = 11
        LNC = 2 * C + 1

        @block.tensor
        def _(pe):
            reader = {}

            def take(bank):
                if bank in reader:
                    pe.wait_ge(*reader.pop(bank))

            def split3(dst, w_hi, w_lo, m_hi, m_lo):
                nc.tensor.matmul(dst, w_hi, m_hi, start=True, stop=False)
                nc.tensor.matmul(dst, w_hi, m_lo, start=False, stop=False)
                return nc.tensor.matmul(dst, w_lo, m_hi, start=False, stop=True)

            pe.wait_ge(mod_in, 32)
            pe.wait_ge(sct_ready, 1)
            for i, j in ((SA, 0), (CA, 1), (SB, 3), (CB, 4)):
                mm = nc.tensor.matmul(M[:, i * NB:(i + 1) * NB], wmod_sb[:, j, :], sct[:], start=True, stop=True)
            mm.then_inc(mod_ps, 1)
            pe.wait_ge(scb_ready, 1)
            for bank, j in ((O, 2), (V, 5)):
                for b in range(NB):
                    mm = nc.tensor.matmul(tile(bank, b), sc_bc[:, b, :], wmod_sb[:, j, :], start=True, stop=True)
                mm.then_inc(gmod_ps, 1)
            reader["M"] = (mod_ready, 2)
            reader["O"] = (gmod_steps, 1)
            reader["V"] = (gmod_steps, 2)

            def project(bank, w, b):
                return split3(bank, wat_hi[:, w], wat_lo[:, w], h_hi[:, b % 2], h_lo[:, b % 2])

            for g in SLOTS:
                if 0 <= g < NB * U:
                    b, u = divmod(g, U)
                    e, k = divmod(u, KB)
                    if u == 0:
                        pe.wait_ge(h2_lo_ready, b + 1)
                        pe.wait_ge(h2_hi_ready, b + 1)
                    if g == 0:
                        pe.wait_ge(w13_hi_ready, NE)
                        pe.wait_ge(w13_lo_ready, NE)
                    if g >= 2:
                        pe.wait_ge(h1b_ready, g - 1)
                    hid = slice(k * P, (k + 1) * P)
                    split3(H1[g % 2], w13_hi[:, 0, e, hid], w13_lo[:, 0, e, hid], h2_hi[:, b % 2], h2_lo[:, b % 2]).then_inc(h1_ps, 1)
                    if g >= 2:
                        pe.wait_ge(hu_ready, g - 1)
                    split3(H3[g % 2], w13_hi[:, 1, e, hid], w13_lo[:, 1, e, hid], h2_hi[:, b % 2], h2_lo[:, b % 2]).then_inc(h3_ps, 1)

                if (b := at(g, HT)) is not None:
                    if b == 0:
                        pe.wait_ge(cst_in, 16)
                    pe.wait_ge(xn_ready[0], C * (b + 1))
                    take("M")
                    for c in range(C):
                        mm = nc.tensor.transpose(tile(M, c), xn[:, 0, c, :], ident)
                    mm.then_inc(xt_ps, 1)
                    reader["M"] = (h_ready, b + 1)
                if (b := at(g, PK)) is not None:
                    if b == 0:
                        pe.wait_ge(wat_hi_ready, 1)
                        pe.wait_ge(wat_lo_ready, 1)
                    pe.wait_ge(h_hi_ready, b + 1)
                    pe.wait_ge(h_lo_ready, b + 1)
                    take("M")
                    project(M, WK, b).then_inc(k_ps, 1)
                    take("V")
                    project(V, WKR, b).then_inc(k_ps, 1)
                    reader["M"] = (rope_k, 2 * b + 1)
                    reader["V"] = (rope_k, 2 * b + 2)
                if (b := at(g, PQ)) is not None:
                    take("O")
                    project(O, WQ, b).then_inc(q_ps, 1)
                    take("M")
                    project(M, WQR, b).then_inc(q_ps, 1)
                    reader["O"] = (rope_q, 2 * b + 1)
                    reader["M"] = (rope_q, 2 * b + 2)
                if (b := at(g, PG)) is not None:
                    take("V")
                    project(V, WG, b).then_inc(g_ps, 1)
                    reader["V"] = (gate_ready, b + 1)
                for v in range(DH + 2):
                    if (b := at(g, DV0 + v)) is not None:
                        if v < DH:
                            take("V")
                            rep = [w[:, v].rearrange("p h d -> p (h d)") for w in (wv_hi, wv_lo)]
                            if b == 0 and v == 0:
                                pe.wait_ge(wv_ready, 2)
                            split3(V, rep[0], rep[1], h_hi[:, b % 2], h_lo[:, b % 2]).then_inc(v_ps, 1)
                            reader["V"] = (kv_ready, DH * b + v + 1)
                        if v >= 2:
                            if v == 2:
                                take("O")
                            n = DH * b + v - 2
                            pe.wait_ge(qs_ready, n + 1)
                            nc.tensor.matmul(O, gather[:, v - 2, :], qs[:, n % 3], start=(v == 2), stop=(v == DH + 1)).then_inc(o_step, 1)
                if (b := at(g, VAR)) is not None:
                    reader["O"] = (osq_ready, b + 1)
                    pe.wait_ge(osq_ready, b + 1)
                    take("M")
                    for c in range(C):
                        mm = nc.tensor.matmul(M[:, c * H:(c + 1) * H], tile(o_sq, c), mean16, start=True, stop=True)
                    mm.then_inc(var_ps, 1)
                    reader["M"] = (gsd_ready, b + 1)
                if (b := at(g, RST)) is not None:
                    pe.wait_ge(grsbc_ready, b + 1)
                    take("M")
                    for c in range(C):
                        mm = nc.tensor.transpose(tile(M, c), grs_bc[:, c, :], ident)
                    mm.then_inc(grst_ps, 1)
                    reader["M"] = (z1_ready, b + 1)
                if (b := at(g, WO)) is not None:
                    if b == 0:
                        pe.wait_ge(small_in, SMALL)
                    pe.wait_ge(z3_ready, b + 1)
                    take("M")
                    for c in range(C):
                        mm = nc.tensor.matmul(tile(M, c), tile(z3, c), wo_sb[:], start=True, stop=True)
                    mm.then_inc(wo_ps, 1)
                    reader["M"] = (att_ready, b + 1)
                if (b := at(g, LN2)) is not None:
                    pe.wait_ge(xn_ready[1], C * (b + 1))
                    take("M")
                    for c in range(C):
                        mm = nc.tensor.transpose(tile(M, c), xn[:, 1, c, :], ident)
                    mm.then_inc(x2t_ps, 1)
                    reader["M"] = (h2_ready, b + 1)
                if (b := at(g, LOG)) is not None:
                    pe.wait_ge(h2_ready, b + 1)
                    take("M")
                    for c in range(C):
                        mm = nc.tensor.matmul(M[:, c * NE:(c + 1) * NE], tile(h2_t, c), wg_sb[:], start=True, stop=True)
                    mm.then_inc(lg_ps, 1)
                    reader["M"] = (lg_steps, LG * b + 1)
                if (b := at(g, GWT)) is not None:
                    pe.wait_ge(gw_ready, b + 1)
                    take("M")
                    for c in range(C):
                        mm = nc.tensor.transpose(tile(M[0:NE], c), gw[:, b % 2, c, :], ident)
                    mm.then_inc(gwt_ps, 1)
                    reader["M"] = (gwt_ready, b + 1)
                if (b := at(g, B2)) is not None:
                    pe.wait_ge(gwt_ready, b + 1)
                    take("M")
                    for c in range(C):
                        mm = nc.tensor.matmul(tile(M, c), tile(gw_t[0:NE], c), b2_sb[0:NE, :], start=True, stop=True)
                    mm.then_inc(b2_ps, 1)
                    reader["M"] = (acc_set, b + 1)

                if g >= 3 and (g - 3) % KB == 0 and (ex := (g - 3) // KB) < NB * NE:
                    if ex == 0:
                        pe.wait_ge(w2_in, 16)
                    pe.wait_ge(hs_ready, KB * ex + KB)
                    if ex >= 1:
                        pe.wait_ge(yg_ready, ex)
                    for c in range(C):
                        for k in range(KB):
                            mm = nc.tensor.matmul(tile(Y, c), tile(hs[:, (KB * ex + k) % 4], c), w2_sb[:, (ex % NE) * KB + k, :],
                                                  start=(k == 0), stop=(k == KB - 1))
                    mm.then_inc(y_ps, 1)
                if (b := at(g, MIXT)) is not None:
                    pe.wait_ge(acc_step, NE * (b + 1))
                    take("M")
                    for c in range(C):
                        mm = nc.tensor.transpose(tile(M, c), acc[:, b % 2, c, :], ident)
                    mm.then_inc(mixt_ps, 1)
                    reader["M"] = (mixt_ready, b + 1)
                if (b := at(g, FF)) is not None:
                    pe.wait_ge(mixt_ready, b + 1)
                    take("M")
                    for c in range(C):
                        mm = nc.tensor.matmul(tile(M, c), tile(mix_t, c), wf_sb[:], start=True, stop=True)
                    mm.then_inc(ff_ps, 1)
                    reader["M"] = (ffg_ready, b + 1)


        @block.vector
        def _(dve):
            def over(ap):
                return ap.unsqueeze(2).to_broadcast([P, C, NE])

            def token_stats(src, b, which):
                chain, st, mo = ln_chain[which], stats[:, b % 2, which], mv[:, b % 2, which]
                for c in range(C):
                    nc.vector.bn_stats(st[:, c, :], src[:, c, :]).then_inc(chain, 1)
                for c in range(C):
                    dve.wait_ge(chain, LNC * b + c + 1)
                    nc.vector.bn_aggr(mo[:, c, :], st[:, c, :]).then_inc(chain, 1)

            def normalise(src, b, which):
                chain, mo, r = ln_chain[which], mv[:, b % 2, which], rstd[:, b % 2, which]
                dve.wait_ge(sd_ready[which], b + 1)
                nc.vector.reciprocal(r, sd[:, b % 2, which]).then_inc(chain, 1)
                dve.wait_ge(chain, LNC * (b + 1))
                for c in range(C):
                    nc.vector.tensor_scalar(xn[:, which, c, :], src[:, c, :], mo[:, c, 0:1], r[:, c:c + 1],
                                            ALU.subtract, ALU.mult).then_inc(xn_ready[which], 1)

            nc.vector.memset(eps[:], EPS).then_inc(eps_set, 1)
            for g in SLOTS:
                if g == SLOTS[0] + 1:
                    dve.wait_ge(wat_hi_ready, 1)
                    nc.vector.tensor_tensor(wat_lo[:], wat[:], wat_hi[:].bitcast(F32), ALU.subtract).then_inc(wat_lo_ready, 1)
                    dve.wait_ge(mod_ps, 1)
                    m_ps = M[:, 0:4 * NB].rearrange("p (i b) -> p i b", i=4)
                    nc.vector.tensor_scalar(mod[:, 0::2], m_ps[:, 0::2], 0.0, None, ALU.add).then_inc(mod_ready, 1)
                    nc.vector.tensor_scalar(mod[:, 1::2], m_ps[:, 1::2], 1.0, None, ALU.add).then_inc(mod_ready, 1)
                if g == SLOTS[0] + 2:
                    dve.wait_ge(gmod_ps, 2)
                    for j, bank in enumerate((O, V)):
                        nc.vector.tensor_copy(g_raw[:, j], tiled(bank)).then_inc(gmod_steps, 1)
                    dve.wait_ge(gmod_steps, 2)
                    nc.vector.tensor_scalar(g_sign, g_raw, 0.0, 2.0, ALU.is_ge, ALU.mult).then_inc(gmod_steps, 1)
                    dve.wait_ge(gmod_steps, 3)
                    nc.vector.tensor_scalar(g_sign, g_sign, -1.0, None, ALU.add).then_inc(gmod_steps, 1)
                    dve.wait_ge(gmod_steps, 4)
                    nc.vector.tensor_tensor(g_abs, g_sign, g_raw, ALU.mult).then_inc(gmod_steps, 1)
                    dve.wait_ge(gmod_steps, 5)
                    nc.vector.scalar_tensor_tensor(gmod[:], g_abs, 0.25, g_sign, ALU.max, ALU.mult).then_inc(gmod_steps, 1)

                if 0 <= g < NB * U:
                    if g == 0:
                        dve.wait_ge(small_in, SMALL)
                    dve.wait_ge(h3_ps, g + 1)
                    dve.wait_ge(h1b_ready, g + 1)
                    if g >= 2:
                        dve.wait_ge(hs_ready, g - 1)
                    nc.vector.scalar_tensor_tensor(hu[:, g % 2], H3[g % 2], b13[:, 1, g % U:g % U + 1], h1b[:, g % 2],
                                                   ALU.add, ALU.mult).then_inc(hu_ready, 1)

                if (b := at(g, LN1)) is not None:
                    dve.wait_ge(x_in[b], 16)
                    if b == 0:
                        dve.wait_ge(eps_set, 1)
                    token_stats(xs[:, b], b, 0)
                if (b := at(g, NRM1)) is not None:
                    if b >= 1:
                        dve.wait_ge(xt_ps, b)
                    normalise(xs[:, b], b, 0)
                if (b := at(g, HT)) is not None:
                    if b == 0:
                        dve.wait_ge(mod_ready, 2)
                    dve.wait_ge(xt_ps, b + 1)
                    nc.vector.tensor_scalar(h_t[:], M, mod[:, CA, b:b + 1], mod[:, SA, b:b + 1], ALU.mult, ALU.add).then_inc(h_ready, 1)
                    dve.wait_ge(h_ready, b + 1)
                    if b >= 2:
                        dve.wait_ge(v_ps, DH * (b - 1))
                    nc.vector.tensor_copy(h_hi[:, b % 2], h_t[:]).then_inc(h_hi_ready, 1)
                    dve.wait_ge(h_hi_ready, b + 1)
                    nc.vector.tensor_tensor(h_lo[:, b % 2], h_t[:], h_hi[:, b % 2].bitcast(F32), ALU.subtract).then_inc(h_lo_ready, 1)
                if (b := at(g, PK)) is not None:
                    if b == 0:
                        dve.wait_ge(cst_in, 16)
                    if b >= 1:
                        dve.wait_ge(khat_ready, b)
                    for i, (bank, tab) in enumerate(((M, cos), (V, sin))):
                        dve.wait_ge(k_ps, 2 * b + i + 1)
                        nc.vector.tensor_tensor(rope[:, i], bank, tab, ALU.mult).then_inc(rope_k, 1)
                if (b := at(g, PQ)) is not None:
                    if b >= 1:
                        dve.wait_ge(qhat_ready, b)
                    for i, (bank, tab) in enumerate(((O, cos), (M, sin))):
                        dve.wait_ge(q_ps, 2 * b + i + 1)
                        nc.vector.tensor_tensor(rope[:, 2 + i], bank, tab, ALU.mult).then_inc(rope_q, 1)
                for v in range(DH + 1):
                    if (b := at(g, DV0 + v)) is not None:
                        if v >= 1:
                            n = DH * b + v - 1
                            dve.wait_ge(kv_ready, n + 1)
                            if n >= 3:
                                dve.wait_ge(qs_ready, n - 2)
                            nc.vector.tensor_tensor_scan(state[:, n % 3], gamma.to_broadcast([P, S]), kv[:, n % 2], 0.0,
                                                         ALU.mult, ALU.add).then_inc(state_ready, 1)
                        if v < DH:
                            n = DH * b + v
                            dve.wait_ge(v_ps, n + 1)
                            if v == 0:
                                dve.wait_ge(khat_ready, b + 1)
                            if n >= 2:
                                dve.wait_ge(state_ready, n - 1)
                            nc.vector.tensor_tensor(kv[:, n % 2], V, khat[:, b % 2], ALU.mult).then_inc(kv_ready, 1)
                if (b := at(g, RSD)) is not None:
                    dve.wait_ge(gsd_ready, b + 1)
                    nc.vector.reciprocal(grs[:], gsd[:]).then_inc(grs_ready, 1)
                    dve.wait_ge(grs_ready, b + 1)
                    if b >= 1:
                        dve.wait_ge(grst_ps, b)
                    nc.vector.tensor_copy(grs_bc[:].rearrange("p c (h d) -> p (c h) d", d=DH),
                                          grs[:].unsqueeze(2).to_broadcast([P, C * H, DH])).then_inc(grsbc_ready, 1)
                if (b := at(g, RST)) is not None:
                    dve.wait_ge(grst_ps, b + 1)
                    dve.wait_ge(osb_ready, b + 1)
                    nc.vector.tensor_tensor(z1[:], M, o_sb[:], ALU.mult).then_inc(z1_ready, 1)
                    if b == 0:
                        dve.wait_ge(small_in, SMALL)
                    dve.wait_ge(z1_ready, b + 1)
                    nc.vector.tensor_scalar(z2[:], z1[:], gn_sb[:, 0:1], gn_sb[:, 1:2], ALU.mult, ALU.add).then_inc(z2_ready, 1)
                    dve.wait_ge(z2_ready, b + 1)
                    dve.wait_ge(gate_ready, b + 1)
                    if b >= 1:
                        dve.wait_ge(wo_ps, b)
                    nc.vector.tensor_tensor(z3[:], z2[:], gate[:, b % 2], ALU.mult).then_inc(z3_ready, 1)
                if (b := at(g, WO)) is not None:
                    dve.wait_ge(wo_ps, b + 1)
                    dve.wait_ge(gmod_steps, 6)
                    nc.vector.tensor_tensor(att[:], tiled(M), gmod[:, GA, b:b + 1, :].to_broadcast([P, C, D]), ALU.mult).then_inc(att_ready, 1)
                    dve.wait_ge(att_ready, b + 1)
                    if b >= 2:
                        dve.wait_ge(x2f_ready, b - 1)
                    nc.vector.tensor_tensor(x2[:, b % 2], att[:], xs[:, b], ALU.add).then_inc(x2_ready, 1)
                    dve.wait_ge(x2_ready, b + 1)
                    token_stats(x2[:, b % 2], b, 1)
                if (b := at(g, NRM2)) is not None:
                    if b >= 1:
                        dve.wait_ge(x2t_ps, b)
                    normalise(x2[:, b % 2], b, 1)
                if (b := at(g, LN2)) is not None:
                    dve.wait_ge(x2t_ps, b + 1)
                    if b >= 1:
                        dve.wait_ge(lg_ps, b)
                    nc.vector.tensor_scalar(h2_t[:], M, mod[:, CB, b:b + 1], mod[:, SB, b:b + 1], ALU.mult, ALU.add).then_inc(h2_ready, 1)
                    dve.wait_ge(h2_ready, b + 1)
                    if b >= 2:
                        dve.wait_ge(h3_ps, U * (b - 1))
                    nc.vector.tensor_copy(h2_hi[:, b % 2], h2_t[:]).then_inc(h2_hi_ready, 1)
                    dve.wait_ge(h2_hi_ready, b + 1)
                    nc.vector.tensor_tensor(h2_lo[:, b % 2], h2_t[:], h2_hi[:, b % 2].bitcast(F32), ALU.subtract).then_inc(h2_lo_ready, 1)
                if (b := at(g, LOG)) is not None:
                    k = LG * b

                    dve.wait_ge(lg_ps, b + 1)
                    nc.vector.tensor_tensor(lg[:, 0], M[:, 0:C * NE].rearrange("p (c e) -> p c e", c=C),
                                            bg_bc[:].unsqueeze(1).to_broadcast([P, C, NE]), ALU.add).then_inc(lg_steps, 1)
                    dve.wait_ge(lg_steps, k + 1)
                    nc.vector.tensor_reduce(lmax[:], lg[:, 0], AX.X, ALU.max).then_inc(lg_steps, 1)
                    dve.wait_ge(lg_steps, k + 2)
                    nc.vector.tensor_tensor(lg[:, 1], lg[:, 0], over(lmax[:]), ALU.subtract).then_inc(lg_steps, 1)
                if (b := at(g, TOP)) is not None:
                    k = LG * b
                    dve.wait_ge(exp_ready, b + 1)
                    nc.vector.tensor_reduce(lsum[:], lg[:, 2], AX.X, ALU.add).then_inc(lg_steps, 1)
                    dve.wait_ge(lg_steps, k + 4)
                    nc.vector.reciprocal(lrec[:], lsum[:]).then_inc(lg_steps, 1)
                    dve.wait_ge(lg_steps, k + 5)
                    pr = prob[:, b % 2]
                    nc.vector.tensor_tensor(pr, lg[:, 2], over(lrec[:]), ALU.mult).then_inc(lg_steps, 1)
                    dve.wait_ge(lg_steps, k + 6)
                    own = pr.unsqueeze(3).to_broadcast([P, C, NE, NE])
                    other = pr.unsqueeze(2).to_broadcast([P, C, NE, NE])
                    nc.vector.tensor_tensor(cmp[:, 0], other, own, ALU.is_equal).then_inc(lg_steps, 1)
                    nc.vector.tensor_tensor(cmp[:, 1], other, own, ALU.is_gt).then_inc(lg_steps, 1)
                    dve.wait_ge(lg_steps, k + 7)
                    nc.vector.tensor_tensor(cmp[:, 2], cmp[:, 0], later.unsqueeze(1).to_broadcast([P, C, NE, NE]), ALU.mult).then_inc(lg_steps, 1)
                    dve.wait_ge(lg_steps, k + 9)
                    nc.vector.tensor_tensor(cmp[:, 3], cmp[:, 2], cmp[:, 1], ALU.add).then_inc(lg_steps, 1)
                    dve.wait_ge(lg_steps, k + 10)
                    nc.vector.tensor_reduce(rank[:], cmp[:, 3], AX.X, ALU.add).then_inc(lg_steps, 1)
                    dve.wait_ge(lg_steps, k + 11)
                    if b >= 2:
                        dve.wait_ge(yg_ready, NE * (b - 1))
                    nc.vector.scalar_tensor_tensor(gw[:, b % 2], rank[:], float(TOPK), pr, ALU.is_lt, ALU.mult).then_inc(gw_ready, 1)
                if (b := at(g, B2)) is not None:
                    dve.wait_ge(b2_ps, b + 1)
                    if b >= 2:
                        dve.wait_ge(mixt_ps, b - 1)
                    nc.vector.tensor_copy(acc[:, b % 2], tiled(M)).then_inc(acc_set, 1)

                if g >= 4 and (g - 4) % KB == 0 and (ex := (g - 4) // KB) < NB * NE:
                    b, e = divmod(ex, NE)
                    dve.wait_ge(y_ps, ex + 1)
                    if e == 0:
                        dve.wait_ge(gw_ready, b + 1)
                    if ex >= 2:
                        dve.wait_ge(acc_step, ex - 1)
                    nc.vector.tensor_tensor(yg[:, ex % 2], tiled(Y), gw[:, b % 2, :, e:e + 1].to_broadcast([P, C, D]), ALU.mult).then_inc(yg_ready, 1)
                if (b := at(g, FF)) is not None:
                    dve.wait_ge(ff_ps, b + 1)
                    nc.vector.tensor_tensor(ffg[:], tiled(M), gmod[:, GB, b:b + 1, :].to_broadcast([P, C, D]), ALU.mult).then_inc(ffg_ready, 1)
                    dve.wait_ge(ffg_ready, b + 1)
                    dve.wait_ge(x2f_ready, b + 1)
                    nc.vector.tensor_tensor(x2f[:, b % 2], ffg[:], x2f[:, b % 2], ALU.add).then_inc(res_ready, 1)

        @block.scalar
        def _(act):
            act.dma_start(ct_sb[:], c_t).then_inc(mod_in, 16)
            act.dma_start(wmod_sb[:], wmod.rearrange("p (j d) -> p j d", d=D)).then_inc(mod_in, 16)
            act.wait_ge(mod_in, 32)
            nc.scalar.activation(sct[:], ct_sb[:], ACT.Silu).then_inc(sct_ready, 1)
            act.wait_ge(sct_ready, 1)
            nc.scalar.activation(sc_bc[:], sct[:].unsqueeze(2).to_broadcast([P, NB, P]), ACT.Copy).then_inc(scb_ready, 1)
            act.wait_ge(wat_in, 16)
            nc.scalar.activation(wat_hi[:], wat[:], ACT.Copy).then_inc(wat_hi_ready, 1)
            act.wait_ge(wat_hi_ready, 1)
            nc.scalar.activation(wv_hi[:].rearrange("p v h k -> p h v k"), by_head(wat_hi), ACT.Copy).then_inc(wv_ready, 1)
            for n, (src, dst) in enumerate(((w1, 0), (w3, 1))):
                act.dma_start(w13[:, dst], src.rearrange("e d h -> d e h")).then_inc(w13_in, 16)
            act.dma_start(w2_sb[:], w2.rearrange("e (k p) d -> p (e k) d", p=P)).then_inc(w2_in, 16)

            def deviation(b, which):
                act.wait_ge(ln_chain[which], LNC * b + 2 * C)
                nc.scalar.activation(sd[:, b % 2, which], mv[:, b % 2, which, :, 1], ACT.Sqrt, bias=eps[:]).then_inc(sd_ready[which], 1)

            for g in SLOTS:
                if g in range(SPLIT, SPLIT + NE):
                    e = g - SPLIT
                    if e == 0:
                        act.wait_ge(w13_in, 32)
                    nc.scalar.activation(w13_hi[:, :, e], w13[:, :, e], ACT.Copy).then_inc(w13_hi_ready, 1)
                if 0 <= g < NB * U:
                    if g == 0:
                        act.wait_ge(small_in, SMALL)
                    act.wait_ge(h1_ps, g + 1)
                    if g >= 2:
                        act.wait_ge(hu_ready, g - 1)
                    nc.scalar.activation(h1b[:, g % 2], H1[g % 2], ACT.Identity, bias=b13[:, 0, g % U:g % U + 1]).then_inc(h1b_ready, 1)
                if 1 <= g < NB * U + 1:
                    n = g - 1
                    act.wait_ge(hu_ready, n + 1)
                    if n >= 4:
                        act.wait_ge(y_ps, (n - 4) // KB + 1)
                    nc.scalar.activation(hs[:, n % 4], hu[:, n % 2], ACT.Silu).then_inc(hs_ready, 1)
                if (b := at(g, LN1)) is not None:
                    if b == 0:
                        act.wait_ge(eps_set, 1)
                    deviation(b, 0)
                if (b := at(g, PG)) is not None:
                    act.wait_ge(g_ps, b + 1)
                    if b >= 2:
                        act.wait_ge(z3_ready, b - 1)
                    nc.scalar.activation(gate[:, b % 2], V, ACT.Silu).then_inc(gate_ready, 1)
                if (b := at(g, SQ)) is not None:
                    act.wait_ge(o_step, DH * (b + 1))
                    if b >= 1:
                        act.wait_ge(z1_ready, b)
                        act.wait_ge(var_ps, b)
                    nc.scalar.activation(o_sb[:], O, ACT.Copy).then_inc(osb_ready, 1)
                    nc.scalar.activation(o_sq[:], O, ACT.Square).then_inc(osq_ready, 1)
                if (b := at(g, VAR)) is not None:
                    act.wait_ge(var_ps, b + 1)
                    if b >= 1:
                        act.wait_ge(grs_ready, b)
                    nc.scalar.activation(gsd[:], M[:, 0:C * H], ACT.Sqrt, bias=eps[:]).then_inc(gsd_ready, 1)
                if (b := at(g, NRM2)) is not None:
                    deviation(b, 1)
                if (b := at(g, LOG)) is not None:
                    act.wait_ge(lg_steps, LG * b + 3)
                    nc.scalar.activation(lg[:, 2], lg[:, 1], ACT.Exp).then_inc(exp_ready, 1)
                if (b := at(g, GWT)) is not None:
                    act.wait_ge(gwt_ps, b + 1)
                    if b >= 1:
                        act.wait_ge(b2_ps, b)
                    nc.scalar.activation(gw_t[0:NE], M[0:NE], ACT.Copy).then_inc(gwt_ready, 1)
                if (b := at(g, MIXT)) is not None:
                    act.wait_ge(mixt_ps, b + 1)
                    if b >= 1:
                        act.wait_ge(ff_ps, b)
                    nc.scalar.activation(mix_t[:], M, ACT.Copy).then_inc(mixt_ready, 1)

        @block.gpsimd
        def _(pool):
            pool.wait_ge(wat_lo_ready, 1)
            nc.gpsimd.tensor_scalar(wv_lo[:].rearrange("p v h k -> p h v k"), by_head(wat_lo), 1.0, 0.0, ALU.mult, ALU.add).then_inc(wv_ready, 1)
            for g in SLOTS:
                if g in range(SPLIT, SPLIT + NE):
                    e = g - SPLIT
                    pool.wait_ge(w13_hi_ready, e + 1)
                    nc.gpsimd.tensor_tensor(w13_lo[:, :, e], w13[:, :, e], w13_hi[:, :, e].bitcast(F32), ALU.subtract).then_inc(w13_lo_ready, 1)
                if (b := at(g, PK)) is not None:
                    pool.wait_ge(rope_k, 2 * b + 2)
                    if b >= 2:
                        pool.wait_ge(kv_ready, DH * (b - 1))
                    nc.gpsimd.tensor_tensor(khat[:, b % 2], rope[:, 0], rope[:, 1], ALU.add).then_inc(khat_ready, 1)
                if (b := at(g, PQ)) is not None:
                    pool.wait_ge(rope_q, 2 * b + 2)
                    nc.gpsimd.tensor_tensor(qhat[:, b % 2], rope[:, 2], rope[:, 3], ALU.add).then_inc(qhat_ready, 1)
                for v in range(1, DH + 1):
                    if (b := at(g, DV0 + v)) is not None:
                        n = DH * b + v - 1
                        pool.wait_ge(state_ready, n + 1)
                        if v == 1:
                            pool.wait_ge(qhat_ready, b + 1)
                        if n >= 3:
                            pool.wait_ge(o_step, n - 2)
                        nc.gpsimd.tensor_tensor(qs[:, n % 3], state[:, n % 3], qhat[:, b % 2], ALU.mult).then_inc(qs_ready, 1)
                if (b := at(g, LN2)) is not None:
                    if b == 0:
                        pool.wait_ge(small_in, SMALL)
                        pool.wait_ge(gmod_steps, 6)
                        nc.gpsimd.tensor_tensor(gb_bf[:], gmod[:, GB], bf_bc[:].unsqueeze(1).to_broadcast([P, NB, D]), ALU.mult).then_inc(gbbf_ready, 1)
                        pool.wait_ge(gbbf_ready, 1)
                    pool.wait_ge(x2_ready, b + 1)
                    if b >= 2:
                        pool.wait_ge(stored, 16 * (b - 1))
                    nc.gpsimd.tensor_tensor(x2f[:, b % 2], x2[:, b % 2], gb_bf[:, b:b + 1, :].to_broadcast([P, C, D]), ALU.add).then_inc(x2f_ready, 1)
                if g >= 4 and (g - 4) % KB == 0 and (ex := (g - 4) // KB) < NB * NE:
                    b = ex // NE
                    pool.wait_ge(yg_ready, ex + 1)
                    if ex % NE == 0:
                        pool.wait_ge(acc_set, b + 1)
                    else:
                        pool.wait_ge(acc_step, ex)
                    nc.gpsimd.tensor_tensor(acc[:, b % 2], acc[:, b % 2], yg[:, ex % 2], ALU.add).then_inc(acc_step, 1)


def kernel(**inputs):
    import concourse.bacc as bacc
    from concourse.bass_utils import run_bass_kernel_spmd

    a = {k.replace("L0_", ""): np.asarray(v) for k, v in inputs.items()}

    def turned(w):
        return w.reshape(D, H, 2, DH // 2)[:, :, ::-1].reshape(D, D)

    wq, wk = a["attn_Wq"].T, a["attn_Wk"].T
    arrays = {
        "x": a["attn_x"],
        "w_att": np.stack([wk, turned(wk), wq, turned(wq), a["attn_Wg"].T, a["attn_Wv"].T], axis=1),
        "wo_t": a["attn_Wo"].T,
        "gn": np.stack([a["attn_gn_w"], a["attn_gn_b"]], axis=1),
        "w1": a["ffn_W1"], "b1_t": a["ffn_b1"].reshape(U, P).T,
        "w3": a["ffn_W3"], "b3_t": a["ffn_b3"].reshape(U, P).T,
        "w2": a["ffn_W2"], "b2": a["ffn_b2"],
        "wg": a["ffn_Wg"], "bg": a["ffn_bg"].reshape(1, NE),
        "wf": a["ffn_Wf"], "bf": a["ffn_bf"].reshape(1, D),
        "c_t": a["c"].T, "wmod": a["wmod"],
        "consts": shape_constants(),
    }
    arrays = {k: np.ascontiguousarray(v) for k, v in arrays.items()}
    nc = bacc.Bacc("TRN2", target_bir_lowering=False, num_devices=1)
    args = [nc.dram_tensor(k, v.shape, mybir.dt.from_np(v.dtype), kind="ExternalInput").ap() for k, v in arrays.items()]
    args.append(nc.dram_tensor("out", (NB, S, D), F32, kind="ExternalOutput").ap())
    build(nc, *args)
    r = run_bass_kernel_spmd(nc, [arrays], core_ids=[0])
    return r.results[0]["out"]
```

```python
from contextlib import ExitStack

import numpy as np

import concourse.bass as bass
from concourse import mybir

F32 = mybir.dt.float32
F32R = mybir.dt.float32r
ALU = mybir.AluOpType
ACT = mybir.ActivationFunctionType
AX = mybir.AxisListType

P = 128
NB = 4
S = 512
C = S // P
D = 128
H = 16
DH = D // H
NE = 8
HID = 256
KB = HID // P
EPS = 1e-5
TOPK = 2
U = NE * KB
WK, WKR, WQ, WQR, WG, WV = range(6)
SA, CA, SB, CB = range(4)
GA, GB = range(2)


def shape_constants():
    inv_freq = (np.float32(1.0) / np.float32(10000.0) ** (np.arange(0, DH, 2, dtype=np.float32) / np.float32(DH))).astype(np.float32)
    freqs = np.arange(S, dtype=np.float32)[:, None] * inv_freq[None, :]
    emb = np.concatenate([freqs, freqs], axis=-1).astype(np.float64)
    sign = np.where(np.arange(DH) < DH // 2, -1.0, 1.0)
    cos = np.tile(np.cos(emb).T, (H, 1)).astype(np.float32)
    sin = np.tile((np.sin(emb) * sign).T, (H, 1)).astype(np.float32)
    gamma = np.repeat(1.0 - 2.0 ** (-5.0 - np.arange(H)), DH)[:, None].astype(np.float32)
    scale = DH ** -0.5
    row_head, row_dim = np.divmod(np.arange(D), DH)
    gather = np.zeros((D, DH, D))
    for dv in range(DH):
        same = row_head[:, None] == row_head[None, :]
        gather[:, dv, :] = same * ((row_dim[None, :] == dv) - 1.0 / DH) * scale
    mean = (row_head[:, None] == np.arange(H)[None, :]) / DH
    ident = np.eye(P)
    later = np.tile((np.arange(NE)[None, :] > np.arange(NE)[:, None]).reshape(1, -1), (P, 1))
    parts = [ident, cos, sin, mean, gamma, later, gather.reshape(D, -1)]
    return np.ascontiguousarray(np.concatenate(parts, axis=1), dtype=np.float32)


CONST_WIDTHS = [P, S, S, H, 1, NE * NE, DH * D]
CONST_AT = [sum(CONST_WIDTHS[:i]) for i in range(len(CONST_WIDTHS) + 1)]


def build(nc, x, w_att, wo_t, gn, w1, b1_t, w3, b3_t, w2, b2, wg, bg, wf, bf, c_t, wmod, consts, out):
    with ExitStack() as ctx:
        def sb(name, *shape, dt=F32):
            return ctx.enter_context(nc.sbuf_tensor(name, [P, *shape], dt))

        def sem(name):
            return ctx.enter_context(nc.semaphore(name))

        cst = sb("cst", CONST_AT[-1])
        ident, cos, sin, mean16, gamma, later, gather = [cst[:, a:b] for a, b in zip(CONST_AT, CONST_AT[1:])]
        gather = gather.rearrange("p (v d) -> p v d", v=DH)
        later = later.rearrange("p (i j) -> p i j", i=NE)
        wat = sb("wat", 6, D)
        wat_hi = sb("wat_hi", 6, D, dt=F32R)
        wat_lo = sb("wat_lo", 6, D, dt=F32R)
        wv_hi = sb("wv_hi", DH, H, DH, dt=F32R)
        wv_lo = sb("wv_lo", DH, H, DH, dt=F32R)
        wo_sb = sb("wo_sb", D)
        gn_sb = sb("gn_sb", 2)
        w13 = sb("w13", 2, NE, HID)
        w13_hi = sb("w13_hi", 2, NE, HID, dt=F32R)
        w13_lo = sb("w13_lo", 2, NE, HID, dt=F32R)
        b13 = sb("b13", 2, U)
        w2_sb = sb("w2_sb", U, D)
        b2_sb = sb("b2_sb", D)
        wg_sb = sb("wg_sb", NE)
        bg_bc = sb("bg_bc", NE)
        wf_sb = sb("wf_sb", D)
        bf_bc = sb("bf_bc", D)
        ct_sb = sb("ct_sb", NB)
        wmod_sb = sb("wmod_sb", 6, D)
        sct = sb("sct", NB)
        sc_bc = sb("sc_bc", NB, P)
        mod = sb("mod", 4, NB)
        gmod = sb("gmod", 2, NB, D)
        gb_bf = sb("gb_bf", NB, D)
        eps = sb("eps", 1)
        xs = sb("xs", NB, C, D)
        stats = sb("stats", 2, 2, C, 6)
        mv = sb("mv", 2, 2, C, 2)
        sd = sb("sd", 2, 2, C)
        rstd = sb("rstd", 2, 2, C)
        xn = sb("xn", 2, C, D)
        h_t = sb("h_t", S)
        h_hi = sb("h_hi", 2, S, dt=F32R)
        h_lo = sb("h_lo", 2, S, dt=F32R)
        rope = sb("rope", 4, S)
        khat = sb("khat", 2, S)
        qhat = sb("qhat", 2, S)
        gate = sb("gate", 2, S)
        kv = sb("kv", 2, S)
        state = sb("state", 3, S)
        qs = sb("qs", 3, S)
        o_sb = sb("o_sb", S)
        o_sq = sb("o_sq", S)
        gsd = sb("gsd", C * H)
        grs = sb("grs", C * H)
        grs_bc = sb("grs_bc", C, D)
        z1 = sb("z1", S)
        z3 = sb("z3", S)
        att = sb("att", C, D)
        x2 = sb("x2", 2, C, D)
        x2f = sb("x2f", 2, C, D)
        h2_t = sb("h2_t", S)
        h2_hi = sb("h2_hi", 2, S, dt=F32R)
        h2_lo = sb("h2_lo", 2, S, dt=F32R)
        lg = sb("lg", 3, C, NE)
        lmax = sb("lmax", C)
        lsum = sb("lsum", C)
        lrec = sb("lrec", C)
        prob = sb("prob", 2, C, NE)
        cmp = sb("cmp", 5, C, NE, NE)
        rank = sb("rank", C, NE)
        gw = sb("gw", 2, C, NE)
        gw_t = sb("gw_t", S)
        stage = w13[:].rearrange("p w e h -> p (w e h)").rearrange("p (n s) -> p n s", s=S)
        h1b, hu, hs = stage[:, 0:2], stage[:, 2:4], stage[:, 4:8]
        yg = sb("yg", 2, C, D)
        acc = sb("acc", 2, C, D)
        mix_t = sb("mix_t", S)
        ffg = sb("ffg", C, D)
        g_raw, g_sign, g_abs = acc[:], yg[:], x2f[:]
        ps = ctx.enter_context(nc.psum_tensor("ps", [P, 8, S], F32))
        H1, H3, Y, O, V, M = [ps[:, 0, :], ps[:, 1, :]], [ps[:, 2, :], ps[:, 3, :]], ps[:, 4, :], ps[:, 5, :], ps[:, 6, :], ps[:, 7, :]

        def tiled(ap):
            return ap.rearrange("p (c d) -> p c d", c=C)

        def tile(ap, c):
            return ap[:, c * P:(c + 1) * P]

        def by_head(w):
            return w[:, WV].bitcast(F32).rearrange("p (h v) -> p h v", h=H).unsqueeze(3).to_broadcast([P, H, DH, DH])

        x_in = [sem(f"x_in{b}") for b in range(NB)]
        wat_in, cst_in, gather_in, mod_in, w13_in, w2_in, small_in = map(sem, ["wat_in", "cst_in", "gather_in", "mod_in", "w13_in", "w2_in", "small_in"])
        eps_set = sem("eps_set")
        sct_ready, scb_ready, mod_ps, mod_ready, gmod_ps, gmod_steps, gbbf_ready = map(sem, [
            "sct_ready", "scb_ready", "mod_ps", "mod_ready", "gmod_ps", "gmod_steps", "gbbf_ready"])
        wv_ready = sem("wv_ready")
        wat_hi_ready, wat_lo_ready, w13_hi_ready, w13_lo_ready = map(sem, ["wat_hi_ready", "wat_lo_ready", "w13_hi_ready", "w13_lo_ready"])
        ln_chain = [sem("ln1_chain"), sem("ln2_chain")]
        sd_ready = [sem("sd1_ready"), sem("sd2_ready")]
        xn_ready = [sem("xn1_ready"), sem("xn2_ready")]
        xt_ps = sem("xt_ps")
        h_ready, h_hi_ready, h_lo_ready = map(sem, ["h_ready", "h_hi_ready", "h_lo_ready"])
        k_ps, q_ps, g_ps, rope_k, rope_q, khat_ready, qhat_ready, gate_ready = map(sem, [
            "k_ps", "q_ps", "g_ps", "rope_k", "rope_q", "khat_ready", "qhat_ready", "gate_ready"])
        v_ps, kv_ready, state_ready, qs_ready, o_step = map(sem, ["v_ps", "kv_ready", "state_ready", "qs_ready", "o_step"])
        osb_ready, osq_ready, var_ps, gsd_ready, grs_ready, grsbc_ready, grst_ps = map(sem, [
            "osb_ready", "osq_ready", "var_ps", "gsd_ready", "grs_ready", "grsbc_ready", "grst_ps"])
        z1_ready, z3_ready, wo_ps, att_ready, x2_ready, x2f_ready = map(sem, [
            "z1_ready", "z3_ready", "wo_ps", "att_ready", "x2_ready", "x2f_ready"])
        x2t_ps, h2_ready, h2_hi_ready, h2_lo_ready = map(sem, ["x2t_ps", "h2_ready", "h2_hi_ready", "h2_lo_ready"])
        lg_ps, lg_steps, exp_ready, ahead_ready, gw_ready, gwt_ps, gwt_ready, b2_ps, acc_set = map(sem, [
            "lg_ps", "lg_steps", "exp_ready", "ahead_ready", "gw_ready", "gwt_ps", "gwt_ready", "b2_ps", "acc_set"])
        h1_ps, h3_ps, h1b_ready, hu_ready, hs_ready, y_ps, yg_ready, acc_step = map(sem, [
            "h1_ps", "h3_ps", "h1b_ready", "hu_ready", "hs_ready", "y_ps", "yg_ready", "acc_step"])
        mixt_ps, mixt_ready, ff_ps, ffg_ready, res_ready, stored = map(sem, [
            "mixt_ps", "mixt_ready", "ff_ps", "ffg_ready", "res_ready", "stored"])

        LN1, NRM1, HT, PK, PQ, PG, DV0 = -2, -1, 0, 1, 2, 3, 4
        SQ = DV0 + DH + 1
        VAR, RSD, RST, WO, NRM2, LN2, LOG, TOP, RANK, GWT, B2 = [SQ + i for i in (1, 2, 6, 7, 8, 9, 10, 11, 12, 13, 14)]
        BACK = [U * b - LOG for b in range(NB)]
        FRONT = [BACK[0] + RST - RSD - 1, -12, BACK[2], BACK[3]]
        MIXT, FF = U + 5, U + 6
        DOWN = 3
        SLOTS = range(FRONT[0] + LN1, NB * U + FF - U + 1)
        SPLIT = FRONT[0] + DV0 + DH + 1

        def at(g, s):
            base = FRONT if s < RST else BACK
            return base.index(g - s) if g - s in base else None

        def closing(g, s):
            b, r = divmod(g - s, U)
            return b if r == 0 and 0 <= b < NB else None

        BANK = {"H10": H1[0], "H11": H1[1], "H30": H3[0], "H31": H3[1], "Y": Y, "O": O, "V": V, "M": M}
        K_BANKS, Q_BANKS = (("H10", "H11"), ("M", "V")), (("H30", "H31"), ("M", "V"))
        AHEAD = 2

        def v_bank(b, v):
            return "Y" if b < AHEAD and v % 2 else "V"

        def each_pair(b):
            pr = prob[:, b % 2]
            return pr.unsqueeze(2).to_broadcast([P, C, NE, NE]), pr.unsqueeze(3).to_broadcast([P, C, NE, NE])

        block = ctx.enter_context(nc.Block())

        @block.sync
        def _(sp):
            sp.dma_start(xs[:, 0], x[0].rearrange("(c p) d -> p c d", p=P)).then_inc(x_in[0], 16)
            sp.dma_start(wat[:], w_att).then_inc(wat_in, 16)
            sp.dma_start(cst[:, :CONST_AT[-2]], consts[:, :CONST_AT[-2]]).then_inc(cst_in, 16)
            sp.dma_start(gather, consts[:, CONST_AT[-2]:].rearrange("p (v d) -> p v d", v=DH)).then_inc(gather_in, 16)
            for dst, src in enumerate((w1, w3)):
                sp.dma_start(w13[:, dst], src.rearrange("e d h -> d e h")).then_inc(w13_in, 16)
            for b in range(1, NB):
                sp.dma_start(xs[:, b], x[b].rearrange("(c p) d -> p c d", p=P)).then_inc(x_in[b], 16)
            sp.dma_start(wo_sb[:], wo_t).then_inc(small_in, 16)
            sp.dma_start(gn_sb[:], gn).then_inc(small_in, 16)
            sp.dma_start(wg_sb[:], wg).then_inc(small_in, 16)
            sp.dma_start(bg_bc[:], bg.to_broadcast([P, NE])).then_inc(small_in, 16)
            sp.dma_start(b2_sb[0:NE, :], b2).then_inc(small_in, 16)
            sp.dma_start(wf_sb[:], wf).then_inc(small_in, 16)
            sp.dma_start(bf_bc[:], bf.to_broadcast([P, D])).then_inc(small_in, 16)
            sp.dma_start(b13[:, 0], b1_t).then_inc(small_in, 16)
            sp.dma_start(b13[:, 1], b3_t).then_inc(small_in, 16)
            sp.dma_start(w2_sb[:], w2.rearrange("e (k p) d -> p (e k) d", p=P)).then_inc(w2_in, 16)
            for b in range(NB):
                sp.wait_ge(res_ready, b + 1)
                sp.dma_start(out[b].rearrange("(c p) d -> p c d", p=P), x2f[:, b % 2]).then_inc(stored, 16)
            sp.wait_ge(stored, 16 * NB)

        SMALL = 9 * 16
        LG = 9
        LNC = 2 * C + 1

        @block.tensor
        def _(pe):
            reader = {}

            def take(bank):
                if bank in reader:
                    pe.wait_ge(*reader.pop(bank))

            def split3(dst, w_hi, w_lo, m_hi, m_lo):
                nc.tensor.matmul(dst, w_hi, m_hi, start=True, stop=False)
                nc.tensor.matmul(dst, w_hi, m_lo, start=False, stop=False)
                return nc.tensor.matmul(dst, w_lo, m_hi, start=False, stop=True)

            pe.wait_ge(mod_in, 32)
            pe.wait_ge(sct_ready, 1)
            for i, j in ((SA, 0), (CA, 1), (SB, 3), (CB, 4)):
                mm = nc.tensor.matmul(M[:, i * NB:(i + 1) * NB], wmod_sb[:, j, :], sct[:], start=True, stop=True)
            mm.then_inc(mod_ps, 1)
            reader["M"] = (mod_ready, 2)

            def project(bank, w, b):
                return split3(bank, wat_hi[:, w], wat_lo[:, w], h_hi[:, b % 2], h_lo[:, b % 2])

            for g in SLOTS:
                if (b := at(g, HT)) is not None:
                    if b == 0:
                        pe.wait_ge(cst_in, 16)
                    pe.wait_ge(xn_ready[0], C * (b + 1))
                    take("M")
                    for c in range(C):
                        mm = nc.tensor.transpose(tile(M, c), xn[:, 0, c, :], ident)
                    mm.then_inc(xt_ps, 1)
                    reader["M"] = (h_ready, b + 1)
                    if b == 0:
                        pe.wait_ge(scb_ready, 1)
                        for bank, j in ((O, 2), (V, 5)):
                            for row in range(NB):
                                mm = nc.tensor.matmul(tile(bank, row), sc_bc[:, row, :], wmod_sb[:, j, :], start=True, stop=True)
                            mm.then_inc(gmod_ps, 1)
                        reader["O"] = (gmod_steps, 1)
                        reader["V"] = (gmod_steps, 2)
                for step, names, weights, done, read in ((PK, K_BANKS, (WK, WKR), k_ps, rope_k), (PQ, Q_BANKS, (WQ, WQR), q_ps, rope_q)):
                    if (b := at(g, step)) is not None:
                        if b == 0 and step == PK:
                            pe.wait_ge(wat_hi_ready, 1)
                            pe.wait_ge(wat_lo_ready, 1)
                        pe.wait_ge(h_hi_ready, b + 1)
                        pe.wait_ge(h_lo_ready, b + 1)
                        for i in range(2):
                            name = names[b >= AHEAD][i]
                            take(name)
                            project(BANK[name], weights[i], b).then_inc(done, 1)
                            reader[name] = (read, 2 * b + 1 + i)
                if (b := at(g, VAR)) is not None:
                    pe.wait_ge(osq_ready, b + 1)
                    take("M")
                    for c in range(C):
                        mm = nc.tensor.matmul(M[:, c * H:(c + 1) * H], tile(o_sq, c), mean16, start=True, stop=True)
                    mm.then_inc(var_ps, 1)
                    reader["M"] = (gsd_ready, b + 1)
                if (b := at(g, RST)) is not None:
                    pe.wait_ge(grsbc_ready, b + 1)
                    take("M")
                    for c in range(C):
                        mm = nc.tensor.transpose(tile(M, c), grs_bc[:, c, :], ident)
                    mm.then_inc(grst_ps, 1)
                    reader["M"] = (z1_ready, b + 1)
                if (b := at(g, WO)) is not None:
                    if b == 0:
                        pe.wait_ge(small_in, SMALL)
                    pe.wait_ge(z3_ready, b + 1)
                    take("M")
                    for c in range(C):
                        mm = nc.tensor.matmul(tile(M, c), tile(z3, c), wo_sb[:], start=True, stop=True)
                    mm.then_inc(wo_ps, 1)
                    reader["M"] = (att_ready, b + 1)
                if (b := at(g, LN2)) is not None:
                    pe.wait_ge(xn_ready[1], C * (b + 1))
                    take("M")
                    for c in range(C):
                        mm = nc.tensor.transpose(tile(M, c), xn[:, 1, c, :], ident)
                    mm.then_inc(x2t_ps, 1)
                    reader["M"] = (h2_ready, b + 1)
                if (b := at(g, LOG)) is not None:
                    pe.wait_ge(h2_ready, b + 1)
                    take("M")
                    for c in range(C):
                        mm = nc.tensor.matmul(M[:, c * NE:(c + 1) * NE], tile(h2_t, c), wg_sb[:], start=True, stop=True)
                    mm.then_inc(lg_ps, 1)
                    reader["M"] = (lg_steps, LG * b + 1)
                if (b := at(g, GWT)) is not None:
                    pe.wait_ge(gw_ready, b + 1)
                    take("M")
                    for c in range(C):
                        mm = nc.tensor.transpose(tile(M[0:NE], c), gw[:, b % 2, c, :], ident)
                    mm.then_inc(gwt_ps, 1)
                    reader["M"] = (gwt_ready, b + 1)
                if (b := at(g, B2)) is not None:
                    pe.wait_ge(gwt_ready, b + 1)
                    take("M")
                    for c in range(C):
                        mm = nc.tensor.matmul(tile(M, c), tile(gw_t[0:NE], c), b2_sb[0:NE, :], start=True, stop=True)
                    mm.then_inc(b2_ps, 1)
                    reader["M"] = (acc_set, b + 1)
                if (b := closing(g, MIXT)) is not None:
                    pe.wait_ge(acc_step, NE * (b + 1))
                    take("M")
                    for c in range(C):
                        mm = nc.tensor.transpose(tile(M, c), acc[:, b % 2, c, :], ident)
                    mm.then_inc(mixt_ps, 1)
                    reader["M"] = (mixt_ready, b + 1)
                if (b := closing(g, FF)) is not None:
                    pe.wait_ge(mixt_ready, b + 1)
                    take("M")
                    for c in range(C):
                        mm = nc.tensor.matmul(tile(M, c), tile(mix_t, c), wf_sb[:], start=True, stop=True)
                    mm.then_inc(ff_ps, 1)
                    reader["M"] = (ffg_ready, b + 1)

                if (b := at(g, PG)) is not None:
                    take("V")
                    project(V, WG, b).then_inc(g_ps, 1)
                    reader["V"] = (gate_ready, b + 1)
                for v in range(DH + 2):
                    if (b := at(g, DV0 + v)) is not None:
                        if v < DH:
                            name = v_bank(b, v)
                            take(name)
                            rep = [w[:, v].rearrange("p h d -> p (h d)") for w in (wv_hi, wv_lo)]
                            if b == 0 and v == 0:
                                pe.wait_ge(wv_ready, 2)
                            split3(BANK[name], rep[0], rep[1], h_hi[:, b % 2], h_lo[:, b % 2]).then_inc(v_ps, 1)
                            reader[name] = (kv_ready, DH * b + v + 1)
                        if v >= 2:
                            if v == 2:
                                take("O")
                            if b == 0 and v == 2:
                                pe.wait_ge(gather_in, 16)
                            n = DH * b + v - 2
                            pe.wait_ge(qs_ready, n + 1)
                            nc.tensor.matmul(O, gather[:, v - 2, :], qs[:, n % 3], start=(v == 2), stop=(v == DH + 1)).then_inc(o_step, 1)
                            if v == DH + 1:
                                reader["O"] = (osb_ready, b + 1)

                if 0 <= g < NB * U:
                    b, u = divmod(g, U)
                    e, k = divmod(u, KB)
                    if u == 0:
                        pe.wait_ge(h2_lo_ready, b + 1)
                        pe.wait_ge(h2_hi_ready, b + 1)
                    if g == 0:
                        pe.wait_ge(w13_hi_ready, NE)
                        pe.wait_ge(w13_lo_ready, NE)
                    if g < 2:
                        take(f"H1{g}")
                    else:
                        pe.wait_ge(h1b_ready, g - 1)
                    hid = slice(k * P, (k + 1) * P)
                    split3(H1[g % 2], w13_hi[:, 0, e, hid], w13_lo[:, 0, e, hid], h2_hi[:, b % 2], h2_lo[:, b % 2]).then_inc(h1_ps, 1)
                    if g < 2:
                        take(f"H3{g}")
                    else:
                        pe.wait_ge(hu_ready, g - 1)
                    split3(H3[g % 2], w13_hi[:, 1, e, hid], w13_lo[:, 1, e, hid], h2_hi[:, b % 2], h2_lo[:, b % 2]).then_inc(h3_ps, 1)

                if g >= DOWN and (g - DOWN) % KB == 0 and (ex := (g - DOWN) // KB) < NB * NE:
                    pe.wait_ge(hs_ready, KB * ex + KB)
                    if ex == 0:
                        pe.wait_ge(w2_in, 16)
                        take("Y")
                    else:
                        pe.wait_ge(yg_ready, ex)
                    for c in range(C):
                        for k in range(KB):
                            mm = nc.tensor.matmul(tile(Y, c), tile(hs[:, (KB * ex + k) % 4], c), w2_sb[:, (ex % NE) * KB + k, :],
                                                  start=(k == 0), stop=(k == KB - 1))
                    mm.then_inc(y_ps, 1)

        @block.vector
        def _(dve):
            def over(ap):
                return ap.unsqueeze(2).to_broadcast([P, C, NE])

            def token_stats(src, b, which):
                chain, st, mo = ln_chain[which], stats[:, b % 2, which], mv[:, b % 2, which]
                for c in range(C):
                    nc.vector.bn_stats(st[:, c, :], src[:, c, :]).then_inc(chain, 1)
                for c in range(C):
                    dve.wait_ge(chain, LNC * b + c + 1)
                    nc.vector.bn_aggr(mo[:, c, :], st[:, c, :]).then_inc(chain, 1)

            def normalise(src, b, which):
                chain, mo, r = ln_chain[which], mv[:, b % 2, which], rstd[:, b % 2, which]
                dve.wait_ge(sd_ready[which], b + 1)
                nc.vector.reciprocal(r, sd[:, b % 2, which]).then_inc(chain, 1)
                dve.wait_ge(chain, LNC * (b + 1))
                for c in range(C):
                    nc.vector.tensor_scalar(xn[:, which, c, :], src[:, c, :], mo[:, c, 0:1], r[:, c:c + 1],
                                            ALU.subtract, ALU.mult).then_inc(xn_ready[which], 1)

            nc.vector.memset(eps[:], EPS).then_inc(eps_set, 1)
            for g in SLOTS:
                if 1 <= g < NB * U + 1:
                    n = g - 1
                    if n == 0:
                        dve.wait_ge(small_in, SMALL)
                    dve.wait_ge(h3_ps, n + 1)
                    dve.wait_ge(h1b_ready, n + 1)
                    if n >= 2:
                        dve.wait_ge(hs_ready, n - 1)
                    nc.vector.scalar_tensor_tensor(hu[:, n % 2], H3[n % 2], b13[:, 1, n % U:n % U + 1], h1b[:, n % 2],
                                                   ALU.add, ALU.mult).then_inc(hu_ready, 1)
                if g > DOWN and (g - DOWN - 1) % KB == 0 and (ex := (g - DOWN - 1) // KB) < NB * NE:
                    b, e = divmod(ex, NE)
                    dve.wait_ge(y_ps, ex + 1)
                    if e == 0:
                        dve.wait_ge(gw_ready, b + 1)
                    if ex >= 2:
                        dve.wait_ge(acc_step, ex - 1)
                    nc.vector.tensor_tensor(yg[:, ex % 2], tiled(Y), gw[:, b % 2, :, e:e + 1].to_broadcast([P, C, D]), ALU.mult).then_inc(yg_ready, 1)

                if (b := at(g, HT)) is not None:
                    if b == 0:
                        dve.wait_ge(mod_ps, 1)
                        m_ps = M[:, 0:4 * NB].rearrange("p (i b) -> p i b", i=4)
                        nc.vector.tensor_scalar(mod[:, 0::2], m_ps[:, 0::2], 0.0, None, ALU.add).then_inc(mod_ready, 1)
                        nc.vector.tensor_scalar(mod[:, 1::2], m_ps[:, 1::2], 1.0, None, ALU.add).then_inc(mod_ready, 1)
                        dve.wait_ge(mod_ready, 2)
                    dve.wait_ge(xt_ps, b + 1)
                    nc.vector.tensor_scalar(h_t[:], M, mod[:, CA, b:b + 1], mod[:, SA, b:b + 1], ALU.mult, ALU.add).then_inc(h_ready, 1)
                    dve.wait_ge(h_ready, b + 1)
                    if b >= 2:
                        dve.wait_ge(v_ps, DH * (b - 1))
                    nc.vector.tensor_copy(h_hi[:, b % 2], h_t[:]).then_inc(h_hi_ready, 1)
                    dve.wait_ge(h_hi_ready, b + 1)
                    nc.vector.tensor_tensor(h_lo[:, b % 2], h_t[:], h_hi[:, b % 2].bitcast(F32), ALU.subtract).then_inc(h_lo_ready, 1)
                    if b == 0:
                        dve.wait_ge(wat_hi_ready, 1)
                        nc.vector.tensor_tensor(wat_lo[:], wat[:], wat_hi[:].bitcast(F32), ALU.subtract).then_inc(wat_lo_ready, 1)
                        dve.wait_ge(gmod_ps, 2)
                        for j, bank in enumerate((O, V)):
                            nc.vector.tensor_copy(g_raw[:, j], tiled(bank)).then_inc(gmod_steps, 1)
                for step, names, done, read, used, part in ((PK, K_BANKS, k_ps, rope_k, khat_ready, 0), (PQ, Q_BANKS, q_ps, rope_q, qhat_ready, 2)):
                    if (b := at(g, step)) is not None:
                        if b == 0:
                            dve.wait_ge(cst_in, 16)
                        if b >= 1:
                            dve.wait_ge(used, b)
                        for i, tab in enumerate((cos, sin)):
                            dve.wait_ge(done, 2 * b + i + 1)
                            nc.vector.tensor_tensor(rope[:, part + i], BANK[names[b >= AHEAD][i]], tab, ALU.mult).then_inc(read, 1)
                if at(g, PG) == 0:
                    dve.wait_ge(gmod_steps, 2)
                    nc.vector.tensor_scalar(g_sign, g_raw, 0.0, 2.0, ALU.is_ge, ALU.mult).then_inc(gmod_steps, 1)
                    dve.wait_ge(gmod_steps, 3)
                    nc.vector.tensor_scalar(g_sign, g_sign, -1.0, None, ALU.add).then_inc(gmod_steps, 1)
                if at(g, VAR) == 0:
                    dve.wait_ge(gmod_steps, 4)
                    nc.vector.tensor_tensor(g_abs, g_sign, g_raw, ALU.mult).then_inc(gmod_steps, 1)
                    dve.wait_ge(gmod_steps, 5)
                    nc.vector.scalar_tensor_tensor(gmod[:], g_abs, 0.25, g_sign, ALU.max, ALU.mult).then_inc(gmod_steps, 1)
                    dve.wait_ge(small_in, SMALL)
                if (b := at(g, RST)) is not None:
                    dve.wait_ge(grst_ps, b + 1)
                    dve.wait_ge(osb_ready, b + 1)
                    nc.vector.tensor_tensor(z1[:], M, o_sb[:], ALU.mult).then_inc(z1_ready, 1)
                    dve.wait_ge(z1_ready, b + 1)
                    dve.wait_ge(gate_ready, b + 1)
                    if b >= 1:
                        dve.wait_ge(wo_ps, b)
                    nc.vector.scalar_tensor_tensor(z3[:], z1[:], gn_sb[:, 1:2], gate[:, b % 2], ALU.add, ALU.mult).then_inc(z3_ready, 1)
                if (b := at(g, WO)) is not None:
                    dve.wait_ge(wo_ps, b + 1)
                    dve.wait_ge(gmod_steps, 6)
                    nc.vector.tensor_tensor(att[:], tiled(M), gmod[:, GA, b:b + 1, :].to_broadcast([P, C, D]), ALU.mult).then_inc(att_ready, 1)
                    dve.wait_ge(att_ready, b + 1)
                    if b >= 2:
                        dve.wait_ge(x2f_ready, b - 1)
                    nc.vector.tensor_tensor(x2[:, b % 2], att[:], xs[:, b], ALU.add).then_inc(x2_ready, 1)
                    dve.wait_ge(x2_ready, b + 1)
                    token_stats(x2[:, b % 2], b, 1)
                if (b := at(g, LN2)) is not None:
                    dve.wait_ge(x2t_ps, b + 1)
                    if b >= 1:
                        dve.wait_ge(lg_ps, b)
                    nc.vector.tensor_scalar(h2_t[:], M, mod[:, CB, b:b + 1], mod[:, SB, b:b + 1], ALU.mult, ALU.add).then_inc(h2_ready, 1)
                    dve.wait_ge(h2_ready, b + 1)
                    if b >= 2:
                        dve.wait_ge(h3_ps, U * (b - 1))
                    nc.vector.tensor_copy(h2_hi[:, b % 2], h2_t[:]).then_inc(h2_hi_ready, 1)
                    dve.wait_ge(h2_hi_ready, b + 1)
                    nc.vector.tensor_tensor(h2_lo[:, b % 2], h2_t[:], h2_hi[:, b % 2].bitcast(F32), ALU.subtract).then_inc(h2_lo_ready, 1)
                if (b := at(g, LOG)) is not None:
                    k = LG * b
                    dve.wait_ge(lg_ps, b + 1)
                    nc.vector.tensor_tensor(lg[:, 0], M[:, 0:C * NE].rearrange("p (c e) -> p c e", c=C),
                                            bg_bc[:].unsqueeze(1).to_broadcast([P, C, NE]), ALU.add).then_inc(lg_steps, 1)
                    dve.wait_ge(lg_steps, k + 1)
                    nc.vector.tensor_reduce(lmax[:], lg[:, 0], AX.X, ALU.max).then_inc(lg_steps, 1)
                    dve.wait_ge(lg_steps, k + 2)
                    nc.vector.tensor_tensor(lg[:, 1], lg[:, 0], over(lmax[:]), ALU.subtract).then_inc(lg_steps, 1)
                if (b := at(g, B2)) is not None:
                    dve.wait_ge(b2_ps, b + 1)
                    if b >= 2:
                        dve.wait_ge(mixt_ps, b - 1)
                    nc.vector.tensor_copy(acc[:, b % 2], tiled(M)).then_inc(acc_set, 1)
                if (b := closing(g, FF)) is not None:
                    dve.wait_ge(ff_ps, b + 1)
                    nc.vector.tensor_tensor(ffg[:], tiled(M), gmod[:, GB, b:b + 1, :].to_broadcast([P, C, D]), ALU.mult).then_inc(ffg_ready, 1)
                    dve.wait_ge(ffg_ready, b + 1)
                    dve.wait_ge(x2f_ready, b + 1)
                    nc.vector.tensor_tensor(x2f[:, b % 2], ffg[:], x2f[:, b % 2], ALU.add).then_inc(res_ready, 1)

                for v in range(DH):
                    if (b := at(g, DV0 + v)) is not None:
                        n = DH * b + v
                        dve.wait_ge(v_ps, n + 1)
                        if v == 0:
                            dve.wait_ge(khat_ready, b + 1)
                        if n >= 2:
                            dve.wait_ge(state_ready, n - 1)
                        nc.vector.tensor_tensor(kv[:, n % 2], BANK[v_bank(b, v)], khat[:, b % 2], ALU.mult).then_inc(kv_ready, 1)
                        dve.wait_ge(kv_ready, n + 1)
                        if n >= 3:
                            dve.wait_ge(qs_ready, n - 2)
                        nc.vector.tensor_tensor_scan(state[:, n % 3], gamma.to_broadcast([P, S]), kv[:, n % 2], 0.0,
                                                     ALU.mult, ALU.add).then_inc(state_ready, 1)

                if (b := at(g, LN1)) is not None:
                    dve.wait_ge(x_in[b], 16)
                    token_stats(xs[:, b], b, 0)
                if (b := at(g, NRM1)) is not None:
                    if b >= 1:
                        dve.wait_ge(xt_ps, b)
                    normalise(xs[:, b], b, 0)
                if (b := at(g, RSD)) is not None:
                    dve.wait_ge(gsd_ready, b + 1)
                    nc.vector.reciprocal(grs[:], gsd[:]).then_inc(grs_ready, 1)
                    dve.wait_ge(grs_ready, b + 1)
                    if b >= 1:
                        dve.wait_ge(grst_ps, b)
                    nc.vector.tensor_copy(grs_bc[:].rearrange("p c (h d) -> p (c h) d", d=DH),
                                          grs[:].unsqueeze(2).to_broadcast([P, C * H, DH])).then_inc(grsbc_ready, 1)
                if (b := at(g, NRM2)) is not None:
                    if b >= 1:
                        dve.wait_ge(x2t_ps, b)
                    normalise(x2[:, b % 2], b, 1)
                if (b := at(g, TOP)) is not None:
                    k = LG * b
                    dve.wait_ge(exp_ready, b + 1)
                    nc.vector.tensor_reduce(lsum[:], lg[:, 2], AX.X, ALU.add).then_inc(lg_steps, 1)
                    dve.wait_ge(lg_steps, k + 4)
                    nc.vector.reciprocal(lrec[:], lsum[:]).then_inc(lg_steps, 1)
                    dve.wait_ge(lg_steps, k + 5)
                    nc.vector.tensor_tensor(prob[:, b % 2], lg[:, 2], over(lrec[:]), ALU.mult).then_inc(lg_steps, 1)
                    dve.wait_ge(lg_steps, k + 6)
                    if b >= 1:
                        dve.wait_ge(ahead_ready, 2 * b)
                    nc.vector.tensor_tensor(cmp[:, 0], *each_pair(b), ALU.is_equal).then_inc(lg_steps, 1)
                    nc.vector.tensor_tensor(cmp[:, 1], *each_pair(b), ALU.is_gt).then_inc(lg_steps, 1)
                if (b := at(g, RANK)) is not None:
                    k = LG * b
                    dve.wait_ge(ahead_ready, 2 * b + 2)
                    nc.vector.tensor_reduce(rank[:], cmp[:, 3], AX.X, ALU.add).then_inc(lg_steps, 1)
                    dve.wait_ge(lg_steps, k + 9)
                    if b >= 2:
                        dve.wait_ge(yg_ready, NE * (b - 1))
                    nc.vector.scalar_tensor_tensor(gw[:, b % 2], rank[:], float(TOPK), prob[:, b % 2], ALU.is_lt, ALU.mult).then_inc(gw_ready, 1)

        @block.scalar
        def _(act):
            act.dma_start(ct_sb[:], c_t).then_inc(mod_in, 16)
            act.dma_start(wmod_sb[:], wmod.rearrange("p (j d) -> p j d", d=D)).then_inc(mod_in, 16)
            act.wait_ge(mod_in, 32)
            nc.scalar.activation(sct[:], ct_sb[:], ACT.Silu).then_inc(sct_ready, 1)
            act.wait_ge(sct_ready, 1)
            nc.scalar.activation(sc_bc[:], sct[:].unsqueeze(2).to_broadcast([P, NB, P]), ACT.Copy).then_inc(scb_ready, 1)

            def deviation(b, which):
                act.wait_ge(ln_chain[which], LNC * b + 2 * C)
                nc.scalar.activation(sd[:, b % 2, which], mv[:, b % 2, which, :, 1], ACT.Sqrt, bias=eps[:]).then_inc(sd_ready[which], 1)

            for g in SLOTS:
                if (b := at(g, NRM1)) is not None:
                    if b == 0:
                        act.wait_ge(eps_set, 1)
                    deviation(b, 0)
                if (b := at(g, NRM2)) is not None:
                    deviation(b, 1)
                if (b := at(g, TOP)) is not None:
                    act.wait_ge(lg_steps, LG * b + 3)
                    nc.scalar.activation(lg[:, 2], lg[:, 1], ACT.Exp).then_inc(exp_ready, 1)

                if 1 <= g < NB * U + 1:
                    n = g - 1
                    if n == 0:
                        act.wait_ge(small_in, SMALL)
                    act.wait_ge(h1_ps, n + 1)
                    if n >= 2:
                        act.wait_ge(hu_ready, n - 1)
                    nc.scalar.activation(h1b[:, n % 2], H1[n % 2], ACT.Identity, bias=b13[:, 0, n % U:n % U + 1]).then_inc(h1b_ready, 1)
                if 2 <= g < NB * U + 2:
                    n = g - 2
                    act.wait_ge(hu_ready, n + 1)
                    if n >= 4:
                        act.wait_ge(y_ps, (n - 4) // KB + 1)
                    nc.scalar.activation(hs[:, n % 4], hu[:, n % 2], ACT.Silu).then_inc(hs_ready, 1)

                if g == FRONT[0] + HT:
                    act.wait_ge(wat_in, 16)
                    nc.scalar.activation(wat_hi[:], wat[:], ACT.Copy).then_inc(wat_hi_ready, 1)
                    act.wait_ge(wat_hi_ready, 1)
                    nc.scalar.activation(wv_hi[:].rearrange("p v h k -> p h v k"), by_head(wat_hi), ACT.Copy).then_inc(wv_ready, 1)
                if g in range(SPLIT, SPLIT + NE):
                    e = g - SPLIT
                    if e == 0:
                        act.wait_ge(w13_in, 32)
                    nc.scalar.activation(w13_hi[:, :, e], w13[:, :, e], ACT.Copy).then_inc(w13_hi_ready, 1)
                if (b := at(g, PG)) is not None:
                    act.wait_ge(g_ps, b + 1)
                    if b >= 2:
                        act.wait_ge(z3_ready, b - 1)
                    nc.scalar.activation(gate[:, b % 2], V, ACT.Silu).then_inc(gate_ready, 1)
                if (b := at(g, SQ)) is not None:
                    if b == 0:
                        act.wait_ge(small_in, SMALL)
                    act.wait_ge(o_step, DH * (b + 1))
                    if b >= 1:
                        act.wait_ge(z1_ready, b)
                        act.wait_ge(var_ps, b)
                    nc.scalar.activation(o_sq[:], O, ACT.Square).then_inc(osq_ready, 1)
                    nc.scalar.activation(o_sb[:], O, ACT.Copy, scale=gn_sb[:, 0:1]).then_inc(osb_ready, 1)
                if (b := at(g, VAR)) is not None:
                    act.wait_ge(var_ps, b + 1)
                    if b >= 1:
                        act.wait_ge(grs_ready, b)
                    nc.scalar.activation(gsd[:], M[:, 0:C * H], ACT.Sqrt, bias=eps[:]).then_inc(gsd_ready, 1)
                if (b := at(g, GWT)) is not None:
                    act.wait_ge(gwt_ps, b + 1)
                    if b >= 1:
                        act.wait_ge(b2_ps, b)
                    nc.scalar.activation(gw_t[0:NE], M[0:NE], ACT.Copy).then_inc(gwt_ready, 1)
                if (b := closing(g, MIXT)) is not None:
                    act.wait_ge(mixt_ps, b + 1)
                    if b >= 1:
                        act.wait_ge(ff_ps, b)
                    nc.scalar.activation(mix_t[:], M, ACT.Copy).then_inc(mixt_ready, 1)

        @block.gpsimd
        def _(pool):
            for g in SLOTS:
                if (b := at(g, PK)) is not None:
                    pool.wait_ge(rope_k, 2 * b + 2)
                    if b >= 2:
                        pool.wait_ge(kv_ready, DH * (b - 1))
                    nc.gpsimd.tensor_tensor(khat[:, b % 2], rope[:, 0], rope[:, 1], ALU.add).then_inc(khat_ready, 1)
                if g == FRONT[0] + PK:
                    pool.wait_ge(wat_lo_ready, 1)
                    nc.gpsimd.tensor_scalar(wv_lo[:].rearrange("p v h k -> p h v k"), by_head(wat_lo), 1.0, 0.0, ALU.mult, ALU.add).then_inc(wv_ready, 1)
                if (b := at(g, PQ)) is not None:
                    pool.wait_ge(rope_q, 2 * b + 2)
                    nc.gpsimd.tensor_tensor(qhat[:, b % 2], rope[:, 2], rope[:, 3], ALU.add).then_inc(qhat_ready, 1)
                for v in range(1, DH + 1):
                    if (b := at(g, DV0 + v)) is not None:
                        n = DH * b + v - 1
                        pool.wait_ge(state_ready, n + 1)
                        if v == 1:
                            pool.wait_ge(qhat_ready, b + 1)
                        if n >= 3:
                            pool.wait_ge(o_step, n - 2)
                        nc.gpsimd.tensor_tensor(qs[:, n % 3], state[:, n % 3], qhat[:, b % 2], ALU.mult).then_inc(qs_ready, 1)
                if g in range(SPLIT, SPLIT + NE):
                    e = g - SPLIT
                    pool.wait_ge(w13_hi_ready, e + 1)
                    nc.gpsimd.tensor_tensor(w13_lo[:, :, e], w13[:, :, e], w13_hi[:, :, e].bitcast(F32), ALU.subtract).then_inc(w13_lo_ready, 1)
                if (b := at(g, NRM2)) is not None:
                    if b == 0:
                        pool.wait_ge(small_in, SMALL)
                        pool.wait_ge(gmod_steps, 6)
                        nc.gpsimd.tensor_tensor(gb_bf[:], gmod[:, GB], bf_bc[:].unsqueeze(1).to_broadcast([P, NB, D]), ALU.mult).then_inc(gbbf_ready, 1)
                        pool.wait_ge(gbbf_ready, 1)
                    pool.wait_ge(x2_ready, b + 1)
                    if b >= 2:
                        pool.wait_ge(stored, 16 * (b - 1))
                    nc.gpsimd.tensor_tensor(x2f[:, b % 2], x2[:, b % 2], gb_bf[:, b:b + 1, :].to_broadcast([P, C, D]), ALU.add).then_inc(x2f_ready, 1)
                if (b := at(g, TOP)) is not None:
                    pool.wait_ge(lg_steps, LG * b + 7)
                    if b >= 1:
                        pool.wait_ge(lg_steps, LG * b)
                    nc.gpsimd.tensor_tensor(cmp[:, 2], cmp[:, 0], later.unsqueeze(1).to_broadcast([P, C, NE, NE]), ALU.mult).then_inc(ahead_ready, 1)
                    pool.wait_ge(ahead_ready, 2 * b + 1)
                    pool.wait_ge(lg_steps, LG * b + 8)
                    nc.gpsimd.tensor_tensor(cmp[:, 3], cmp[:, 2], cmp[:, 1], ALU.add).then_inc(ahead_ready, 1)
                if g > DOWN and (g - DOWN - 1) % KB == 0 and (ex := (g - DOWN - 1) // KB) < NB * NE:
                    b = ex // NE
                    pool.wait_ge(yg_ready, ex + 1)
                    if ex % NE == 0:
                        pool.wait_ge(acc_set, b + 1)
                    else:
                        pool.wait_ge(acc_step, ex)
                    nc.gpsimd.tensor_tensor(acc[:, b % 2], acc[:, b % 2], yg[:, ex % 2], ALU.add).then_inc(acc_step, 1)


def kernel(**inputs):
    import concourse.bacc as bacc
    from concourse.bass_utils import run_bass_kernel_spmd

    a = {k.replace("L0_", ""): np.asarray(v) for k, v in inputs.items()}

    def turned(w):
        return w.reshape(D, H, 2, DH // 2)[:, :, ::-1].reshape(D, D)

    wq, wk = a["attn_Wq"].T, a["attn_Wk"].T
    arrays = {
        "x": a["attn_x"],
        "w_att": np.stack([wk, turned(wk), wq, turned(wq), a["attn_Wg"].T, a["attn_Wv"].T], axis=1),
        "wo_t": a["attn_Wo"].T,
        "gn": np.stack([a["attn_gn_w"], a["attn_gn_b"]], axis=1),
        "w1": a["ffn_W1"], "b1_t": a["ffn_b1"].reshape(U, P).T,
        "w3": a["ffn_W3"], "b3_t": a["ffn_b3"].reshape(U, P).T,
        "w2": a["ffn_W2"], "b2": a["ffn_b2"],
        "wg": a["ffn_Wg"], "bg": a["ffn_bg"].reshape(1, NE),
        "wf": a["ffn_Wf"], "bf": a["ffn_bf"].reshape(1, D),
        "c_t": a["c"].T, "wmod": a["wmod"],
        "consts": shape_constants(),
    }
    arrays = {k: np.ascontiguousarray(v) for k, v in arrays.items()}
    nc = bacc.Bacc("TRN2", target_bir_lowering=False, num_devices=1)
    args = [nc.dram_tensor(k, v.shape, mybir.dt.from_np(v.dtype), kind="ExternalInput").ap() for k, v in arrays.items()]
    args.append(nc.dram_tensor("out", (NB, S, D), F32, kind="ExternalOutput").ap())
    build(nc, *args)
    r = run_bass_kernel_spmd(nc, [arrays], core_ids=[0])
    return r.results[0]["out"]
```

```python
from contextlib import ExitStack

import numpy as np

import concourse.bass as bass
from concourse import mybir

F32 = mybir.dt.float32
F32R = mybir.dt.float32r
ALU = mybir.AluOpType
ACT = mybir.ActivationFunctionType
AX = mybir.AxisListType

P = 128
NB = 4
S = 512
C = S // P
D = 128
H = 16
DH = D // H
NE = 8
HID = 256
KB = HID // P
EPS = 1e-5
TOPK = 2
U = NE * KB
WK, WKR, WQ, WQR, WG, WV = range(6)
SA, CA, SB, CB = range(4)
GA, GB = range(2)


def shape_constants():
    inv_freq = (np.float32(1.0) / np.float32(10000.0) ** (np.arange(0, DH, 2, dtype=np.float32) / np.float32(DH))).astype(np.float32)
    freqs = np.arange(S, dtype=np.float32)[:, None] * inv_freq[None, :]
    emb = np.concatenate([freqs, freqs], axis=-1).astype(np.float64)
    sign = np.where(np.arange(DH) < DH // 2, -1.0, 1.0)
    cos = np.tile(np.cos(emb).T, (H, 1)).astype(np.float32)
    sin = np.tile((np.sin(emb) * sign).T, (H, 1)).astype(np.float32)
    gamma = np.repeat(1.0 - 2.0 ** (-5.0 - np.arange(H)), DH)[:, None].astype(np.float32)
    row_head, row_dim = np.divmod(np.arange(D), DH)
    gather = np.zeros((D, DH, D))
    for dv in range(DH):
        same = row_head[:, None] == row_head[None, :]
        gather[:, dv, :] = same * ((row_dim[None, :] == dv) - 1.0 / DH)
    mean = (row_head[:, None] == np.arange(H)[None, :]) / DH
    ident = np.eye(P)
    later = np.tile((np.arange(NE)[None, :] > np.arange(NE)[:, None]).reshape(1, -1), (P, 1))
    parts = [ident, cos, sin, mean, gamma, later, gather.reshape(D, -1)]
    return np.ascontiguousarray(np.concatenate(parts, axis=1), dtype=np.float32)


CONST_WIDTHS = [P, S, S, H, 1, NE * NE, DH * D]
SCALING = DH ** -0.5
CONST_AT = [sum(CONST_WIDTHS[:i]) for i in range(len(CONST_WIDTHS) + 1)]


def build(nc, x, w_att, wo_t, gn, w1, b1_t, w3, b3_t, w2_t, b2_t, wg, bg, wf, bf, c_t, wmod, consts, out):
    with ExitStack() as ctx:
        def sb(name, *shape, dt=F32):
            return ctx.enter_context(nc.sbuf_tensor(name, [P, *shape], dt))

        def sem(name):
            return ctx.enter_context(nc.semaphore(name))

        cst = sb("cst", CONST_AT[-2])
        ident, cos, sin, mean16, gamma, later = [cst[:, a:b] for a, b in zip(CONST_AT[:-1], CONST_AT[1:-1])]
        gather = sb("gather", DH, D, dt=F32R)
        later = later.rearrange("p (i j) -> p i j", i=NE)
        wat = sb("wat", 6, D)
        wat_hi = sb("wat_hi", 6, D, dt=F32R)
        wat_lo = sb("wat_lo", 6, D, dt=F32R)
        wv_hi = sb("wv_hi", DH, H, DH, dt=F32R)
        wv_lo = sb("wv_lo", DH, H, DH, dt=F32R)
        wo_sb = sb("wo_sb", D)
        gn_sb = sb("gn_sb", 2)
        gn_scale = sb("gn_scale", 1)
        w13 = sb("w13", 2, NE, HID)
        w13_hi = sb("w13_hi", 2, NE, HID, dt=F32R)
        w13_lo = sb("w13_lo", 2, NE, HID, dt=F32R)
        b13 = sb("b13", 2, U)
        w2f = sb("w2f", U, D)
        b2f = sb("b2f", D)
        b2_sb = sb("b2_sb", NE)
        wg_sb = sb("wg_sb", NE)
        bg_bc = sb("bg_bc", NE)
        wf_sb = sb("wf_sb", D)
        bf_bc = sb("bf_bc", D)
        ct_sb = sb("ct_sb", NB)
        wmod_sb = sb("wmod_sb", 6, D)
        sct = sb("sct", NB)
        mod = sb("mod", 4, NB)
        gcol = sb("gcol", 5, 2, NB)
        gmod = sb("gmod", 2, NB, D)
        gb_bf = sb("gb_bf", NB, D)
        eps = sb("eps", 1)
        xs = sb("xs", NB, C, D)
        stats = sb("stats", 2, 2, C, 6)
        mv = sb("mv", 2, 2, C, 2)
        sd = sb("sd", 2, 2, C)
        rstd = sb("rstd", 2, 2, C)
        xn = sb("xn", 2, C, D)
        h_t = sb("h_t", S)
        h_hi = sb("h_hi", 2, S, dt=F32R)
        h_lo = sb("h_lo", 2, S, dt=F32R)
        rope = sb("rope", 4, S)
        khat = sb("khat", 2, S)
        qhat = sb("qhat", 2, S)
        gate = sb("gate", 2, S)
        kv = sb("kv", 2, S)
        state = sb("state", 3, S)
        qs = sb("qs", 3, S)
        qs_hi = sb("qs_hi", 2, S, dt=F32R)
        qs_lo = sb("qs_lo", 2, S, dt=F32R)
        o_sb = sb("o_sb", S)
        o_sq = sb("o_sq", S)
        gsd = sb("gsd", C * H)
        grs = sb("grs", C * H)
        grs_bc = sb("grs_bc", C, D)
        z1 = sb("z1", S)
        z3 = sb("z3", S)
        att = sb("att", C, D)
        x2 = sb("x2", 2, C, D)
        x2f = sb("x2f", 2, C, D)
        h2_t = sb("h2_t", S)
        h2_hi = sb("h2_hi", 2, S, dt=F32R)
        h2_lo = sb("h2_lo", 2, S, dt=F32R)
        lg = sb("lg", 3, C, NE)
        lmax = sb("lmax", C)
        lsum = sb("lsum", C)
        lrec = sb("lrec", C)
        prob = sb("prob", 2, C, NE)
        cmp = sb("cmp", 4, C, NE, NE)
        gather_stage = cmp[:].rearrange("p n c i j -> p (n c i j)")
        rank = sb("rank", C, NE)
        gw = sb("gw", 2, C, NE)
        gw_t = sb("gw_t", S)
        stage = w13[:].rearrange("p w e h -> p (w e h)").rearrange("p (n s) -> p n s", s=S)
        h1b, hu, hs = stage[:, 0:2], stage[:, 2:4], stage[:, 4:8]
        yg = sb("yg", 2, C, D)
        acc = sb("acc", 2, C, D)
        ffg = sb("ffg", C, D)
        g_rep = x2f
        w2_half = [buf[:].rearrange("p n c d -> p (n c) d") for buf in (acc, yg)]
        ps = ctx.enter_context(nc.psum_tensor("ps", [P, 8, S], F32))
        H1, H3, Y, O, V, M = [ps[:, 0, :], ps[:, 1, :]], [ps[:, 2, :], ps[:, 3, :]], ps[:, 4, :], ps[:, 5, :], ps[:, 6, :], ps[:, 7, :]

        def tiled(ap):
            return ap.rearrange("p (c d) -> p c d", c=C)

        def tile(ap, c):
            return ap[:, c * P:(c + 1) * P]

        def by_head(w):
            return w[:, WV].bitcast(F32).rearrange("p (h v) -> p h v", h=H).unsqueeze(3).to_broadcast([P, H, DH, DH])

        x_in = [sem(f"x_in{b}") for b in range(NB)]
        wat_in, cst_in, gather_in, ct_in, mod_in, w13_in, w2_in, small_in = map(sem, ["wat_in", "cst_in", "gather_in", "ct_in", "mod_in", "w13_in", "w2_in", "small_in"])
        eps_set = sem("eps_set")
        sct_ready, mod_ps, mod_ready, gcol_steps, grep_ready, gmod_ps, gmod_ready, gbbf_ready = map(sem, [
            "sct_ready", "mod_ps", "mod_ready", "gcol_steps", "grep_ready", "gmod_ps", "gmod_ready", "gbbf_ready"])
        wv_ready, gather_ready, gn_ready = map(sem, ["wv_ready", "gather_ready", "gn_ready"])
        wat_hi_ready, wat_lo_ready, w13_hi_ready, w13_lo_ready = map(sem, ["wat_hi_ready", "wat_lo_ready", "w13_hi_ready", "w13_lo_ready"])
        ln_chain = [sem("ln1_chain"), sem("ln2_chain")]
        sd_ready = [sem("sd1_ready"), sem("sd2_ready")]
        xn_ready = [sem("xn1_ready"), sem("xn2_ready")]
        xt_ps = sem("xt_ps")
        h_ready, h_hi_ready, h_lo_ready = map(sem, ["h_ready", "h_hi_ready", "h_lo_ready"])
        k_ps, q_ps, g_ps, rope_k, rope_q, khat_ready, qhat_ready, gate_ready = map(sem, [
            "k_ps", "q_ps", "g_ps", "rope_k", "rope_q", "khat_ready", "qhat_ready", "gate_ready"])
        v_ps, kv_ready, state_ready, qs_ready, qs_hi_ready, qs_lo_ready, o_step = map(sem, ["v_ps", "kv_ready", "state_ready", "qs_ready", "qs_hi_ready", "qs_lo_ready", "o_step"])
        osb_ready, osq_ready, var_ps, gsd_ready, grs_ready, grsbc_ready, grst_ps = map(sem, [
            "osb_ready", "osq_ready", "var_ps", "gsd_ready", "grs_ready", "grsbc_ready", "grst_ps"])
        z1_ready, z3_ready, wo_ps, att_ready, x2_ready, x2f_ready = map(sem, [
            "z1_ready", "z3_ready", "wo_ps", "att_ready", "x2_ready", "x2f_ready"])
        x2t_ps, h2_ready, h2_hi_ready, h2_lo_ready = map(sem, ["x2t_ps", "h2_ready", "h2_hi_ready", "h2_lo_ready"])
        lg_ps, lg_steps, exp_ready, ahead_ready, gw_ready, gwt_ps, gwt_ready, b2_ps, acc_set = map(sem, [
            "lg_ps", "lg_steps", "exp_ready", "ahead_ready", "gw_ready", "gwt_ps", "gwt_ready", "b2_ps", "acc_set"])
        h1_ps, h3_ps, h1b_ready, hu_ready, hs_ready, y_ps, yg_ready, acc_step = map(sem, [
            "h1_ps", "h3_ps", "h1b_ready", "hu_ready", "hs_ready", "y_ps", "yg_ready", "acc_step"])
        w2f_ps, w2f_ready, b2f_ps, b2f_ready, ffg_ready, res_ready, stored = map(sem, [
            "w2f_ps", "w2f_ready", "b2f_ps", "b2f_ready", "ffg_ready", "res_ready", "stored"])

        LN1, NRM1, HT, PK, PQ, PG, DV0 = -3, -2, 0, 1, 2, 3, 4
        SQ = DV0 + DH + 2
        VAR, RSD, RST, WO, NRM2, LN2, LOG, TOP, RANK, GWT, B2 = [SQ + i for i in (1, 2, 5, 6, 7, 9, 10, 11, 12, 13, 14)]
        BACK = [U * b - LOG for b in range(NB)]
        FRONT = [BACK[0] + RST - RSD - 1, -11, BACK[2], BACK[3]]
        SUM = U + 4
        DOWN = 3
        SLOTS = range(FRONT[0] + LN1, NB * U + SUM - U + 1)
        FUSE = RST + BACK[0]
        FUSED = S // D
        ON_VECTOR = 3
        SPLIT_HI = FRONT[0] + PG
        SPLIT_LO = [FRONT[0] + DV0 + DH] * ON_VECTOR + [FRONT[0] + DV0 + 1 + 2 * i for i in range(NE - ON_VECTOR)]

        def at(g, s):
            base = FRONT if s < RST else BACK
            return base.index(g - s) if g - s in base else None

        def closing(g, s):
            b, r = divmod(g - s, U)
            return b if r == 0 and 0 <= b < NB else None

        BANK = {"H10": H1[0], "H11": H1[1], "H30": H3[0], "H31": H3[1], "Y": Y, "O": O, "V": V, "M": M}
        K_BANKS, Q_BANKS = (("H10", "H11"), ("M", "V")), (("H30", "H31"), ("M", "V"))
        AHEAD = 2

        def v_bank(b, v):
            return "Y" if b < AHEAD and v % 2 else "V"

        def each_pair(b):
            pr = prob[:, b % 2]
            return pr.unsqueeze(2).to_broadcast([P, C, NE, NE]), pr.unsqueeze(3).to_broadcast([P, C, NE, NE])

        def row_parts(b):
            return [slice(0, C)] if b < NB - 1 else [slice(0, C // 2), slice(C // 2, C)]

        def parts_before(b, part):
            return b + (part.start > 0)

        block = ctx.enter_context(nc.Block())

        @block.sync
        def _(sp):
            sp.dma_start(xs[:, 0], x[0].rearrange("(c p) d -> p c d", p=P)).then_inc(x_in[0], 16)
            sp.dma_start(wat[:], w_att).then_inc(wat_in, 16)
            sp.dma_start(cst[:, :CONST_AT[-2]], consts[:, :CONST_AT[-2]]).then_inc(cst_in, 16)
            sp.dma_start(gather_stage, consts[:, CONST_AT[-2]:]).then_inc(gather_in, 16)
            for dst, src in enumerate((w1, w3)):
                sp.dma_start(w13[:, dst], src.rearrange("e d h -> d e h")).then_inc(w13_in, 16)
            for b in range(1, NB):
                sp.dma_start(xs[:, b], x[b].rearrange("(c p) d -> p c d", p=P)).then_inc(x_in[b], 16)
            sp.dma_start(wo_sb[:], wo_t).then_inc(small_in, 16)
            sp.dma_start(gn_sb[:], gn).then_inc(small_in, 16)
            sp.dma_start(wg_sb[:], wg).then_inc(small_in, 16)
            sp.dma_start(bg_bc[:], bg.to_broadcast([P, NE])).then_inc(small_in, 16)
            sp.dma_start(b2_sb[:], b2_t).then_inc(small_in, 16)
            sp.dma_start(wf_sb[:], wf).then_inc(small_in, 16)
            sp.dma_start(bf_bc[:], bf.to_broadcast([P, D])).then_inc(small_in, 16)
            sp.dma_start(b13[:, 0], b1_t).then_inc(small_in, 16)
            sp.dma_start(b13[:, 1], b3_t).then_inc(small_in, 16)
            for n, half in enumerate(w2_half):
                sp.dma_start(half, w2_t[:, n * U // 2:(n + 1) * U // 2, :]).then_inc(w2_in, 16)
            for b in range(NB):
                for part in row_parts(b):
                    sp.wait_ge(res_ready, parts_before(b, part) + 1)
                    sp.dma_start(out[b].rearrange("(c p) d -> p c d", p=P)[:, part], x2f[:, b % 2, part]).then_inc(stored, 16)
            sp.wait_ge(stored, 16 * (NB + 1))

        SMALL = 9 * 16
        LG = 9
        LNC = 2 * C + 1

        @block.tensor
        def _(pe):
            reader = {}

            def take(bank):
                if bank in reader:
                    pe.wait_ge(*reader.pop(bank))

            def split3(dst, w_hi, w_lo, m_hi, m_lo):
                nc.tensor.matmul(dst, w_hi, m_hi, start=True, stop=False)
                nc.tensor.matmul(dst, w_hi, m_lo, start=False, stop=False)
                return nc.tensor.matmul(dst, w_lo, m_hi, start=False, stop=True)

            pe.wait_ge(mod_in, 16)
            pe.wait_ge(sct_ready, 1)
            for i, j in ((SA, 0), (CA, 1), (SB, 3), (CB, 4), (4 + GA, 2), (4 + GB, 5)):
                mm = nc.tensor.matmul(Y[:, i * NB:(i + 1) * NB], wmod_sb[:, j, :], sct[:], start=True, stop=True)
            mm.then_inc(mod_ps, 1)
            reader["Y"] = (mod_ready, 3)

            def project(bank, w, b):
                return split3(bank, wat_hi[:, w], wat_lo[:, w], h_hi[:, b % 2], h_lo[:, b % 2])

            def gate_rows(name, j):
                take(name)
                for row in range(NB):
                    mm = nc.tensor.matmul(tile(BANK[name], row), g_rep[:, j, row, :], ident, start=True, stop=True)
                mm.then_inc(gmod_ps, 1)
                reader[name] = (gmod_ready, j + 1)

            for g in SLOTS:
                if (b := at(g, HT)) is not None:
                    if b == 0:
                        pe.wait_ge(cst_in, 16)
                    pe.wait_ge(xn_ready[0], C * (b + 1))
                    take("M")
                    for c in range(C):
                        mm = nc.tensor.transpose(tile(M, c), xn[:, 0, c, :], ident)
                    mm.then_inc(xt_ps, 1)
                    reader["M"] = (h_ready, b + 1)
                    if b == 0:
                        pe.wait_ge(grep_ready, 1)
                        gate_rows("O", GA)
                for step, names, weights, done, read in ((PK, K_BANKS, (WK, WKR), k_ps, rope_k), (PQ, Q_BANKS, (WQ, WQR), q_ps, rope_q)):
                    if (b := at(g, step)) is not None:
                        if b == 0 and step == PK:
                            pe.wait_ge(wat_hi_ready, 1)
                            pe.wait_ge(wat_lo_ready, 1)
                        pe.wait_ge(h_hi_ready, b + 1)
                        pe.wait_ge(h_lo_ready, b + 1)
                        for i in range(2):
                            name = names[b >= AHEAD][i]
                            take(name)
                            project(BANK[name], weights[i], b).then_inc(done, 1)
                            reader[name] = (read, 2 * b + 1 + i)
                if (b := at(g, VAR)) is not None:
                    pe.wait_ge(osq_ready, b + 1)
                    take("M")
                    for c in range(C):
                        mm = nc.tensor.matmul(M[:, c * H:(c + 1) * H], tile(o_sq, c), mean16, start=True, stop=True)
                    mm.then_inc(var_ps, 1)
                    reader["M"] = (gsd_ready, b + 1)
                if (b := at(g, RST)) is not None:
                    pe.wait_ge(grsbc_ready, b + 1)
                    take("M")
                    for c in range(C):
                        mm = nc.tensor.transpose(tile(M, c), grs_bc[:, c, :], ident)
                    mm.then_inc(grst_ps, 1)
                    reader["M"] = (z1_ready, b + 1)
                if (b := at(g, WO)) is not None:
                    if b == 0:
                        pe.wait_ge(small_in, SMALL)
                    pe.wait_ge(z3_ready, b + 1)
                    take("M")
                    for c in range(C):
                        mm = nc.tensor.matmul(tile(M, c), tile(z3, c), wo_sb[:], start=True, stop=True)
                    mm.then_inc(wo_ps, 1)
                    reader["M"] = (att_ready, b + 1)
                if (b := at(g, LN2)) is not None:
                    pe.wait_ge(xn_ready[1], C * (b + 1))
                    take("M")
                    for c in range(C):
                        mm = nc.tensor.transpose(tile(M, c), xn[:, 1, c, :], ident)
                    mm.then_inc(x2t_ps, 1)
                    reader["M"] = (h2_ready, b + 1)
                if (b := at(g, LOG)) is not None:
                    pe.wait_ge(h2_ready, b + 1)
                    take("M")
                    for c in range(C):
                        mm = nc.tensor.matmul(M[:, c * NE:(c + 1) * NE], tile(h2_t, c), wg_sb[:], start=True, stop=True)
                    mm.then_inc(lg_ps, 1)
                    reader["M"] = (lg_steps, LG * b + 1)
                if (b := at(g, GWT)) is not None:
                    pe.wait_ge(gw_ready, b + 1)
                    take("M")
                    for c in range(C):
                        mm = nc.tensor.transpose(tile(M[0:NE], c), gw[:, b % 2, c, :], ident)
                    mm.then_inc(gwt_ps, 1)
                    reader["M"] = (gwt_ready, b + 1)
                if (b := at(g, B2)) is not None:
                    pe.wait_ge(gwt_ready, b + 1)
                    if b == 0:
                        pe.wait_ge(b2f_ready, 1)
                    take("M")
                    for c in range(C):
                        mm = nc.tensor.matmul(tile(M, c), tile(gw_t[0:NE], c), b2f[0:NE, :], start=True, stop=True)
                    mm.then_inc(b2_ps, 1)
                    reader["M"] = (acc_set, b + 1)
                if (n := g - FUSE) in range(U // FUSED):
                    if n == 0:
                        pe.wait_ge(w2_in, 32)
                        pe.wait_ge(small_in, SMALL)
                    name = ("H10", "H30", "H11", "H31")[n]
                    take(name)
                    for i in range(FUSED):
                        unit = n * FUSED + i
                        mm = nc.tensor.matmul(tile(BANK[name], i), w2_half[unit // (U // 2)][:, unit % (U // 2), :], wf_sb[:], start=True, stop=True)
                    mm.then_inc(w2f_ps, 1)
                    reader[name] = (w2f_ready, n + 1)
                    if n == 0:
                        take("M")
                        nc.tensor.matmul(M[0:NE, 0:D], b2_sb[:], wf_sb[:], start=True, stop=True).then_inc(b2f_ps, 1)
                        reader["M"] = (b2f_ready, 1)

                if (b := at(g, PG)) is not None:
                    take("V")
                    project(V, WG, b).then_inc(g_ps, 1)
                    reader["V"] = (gate_ready, b + 1)
                for v in range(DH + 3):
                    if (b := at(g, DV0 + v)) is not None:
                        if v < DH:
                            name = v_bank(b, v)
                            take(name)
                            rep = [w[:, v].rearrange("p h d -> p (h d)") for w in (wv_hi, wv_lo)]
                            if b == 0 and v == 0:
                                pe.wait_ge(wv_ready, 2)
                            split3(BANK[name], rep[0], rep[1], h_hi[:, b % 2], h_lo[:, b % 2]).then_inc(v_ps, 1)
                            reader[name] = (kv_ready, DH * b + v + 1)
                        if b == 0 and v == 1:
                            gate_rows("M", GB)
                        if v >= 3:
                            if v == 3:
                                take("O")
                            if b == 0 and v == 3:
                                pe.wait_ge(gather_ready, 1)
                            n = DH * b + v - 3
                            first, last = v == 3, v == DH + 2
                            if b < AHEAD:
                                pe.wait_ge(qs_ready, n + 1)
                                mm = nc.tensor.matmul(O, gather[:, v - 3, :].bitcast(F32), qs[:, n % 3], start=first, stop=last)
                            else:
                                pe.wait_ge(qs_hi_ready, n - DH * AHEAD + 1)
                                pe.wait_ge(qs_lo_ready, n - DH * AHEAD + 1)
                                nc.tensor.matmul(O, gather[:, v - 3, :], qs_hi[:, n % 2], start=first, stop=False)
                                mm = nc.tensor.matmul(O, gather[:, v - 3, :], qs_lo[:, n % 2], start=False, stop=last)
                            mm.then_inc(o_step, 1)
                            if last:
                                reader["O"] = (osb_ready, b + 1)

                if 0 <= g < NB * U:
                    b, u = divmod(g, U)
                    e, k = divmod(u, KB)
                    if u == 0:
                        pe.wait_ge(h2_lo_ready, b + 1)
                        pe.wait_ge(h2_hi_ready, b + 1)
                    if g == 0:
                        pe.wait_ge(w13_hi_ready, NE)
                        pe.wait_ge(w13_lo_ready, NE)
                    if g < 2:
                        take(f"H1{g}")
                    else:
                        pe.wait_ge(h1b_ready, g - 1)
                    hid = slice(k * P, (k + 1) * P)
                    split3(H1[g % 2], w13_hi[:, 0, e, hid], w13_lo[:, 0, e, hid], h2_hi[:, b % 2], h2_lo[:, b % 2]).then_inc(h1_ps, 1)
                    if g < 2:
                        take(f"H3{g}")
                    else:
                        pe.wait_ge(hu_ready, g - 1)
                    split3(H3[g % 2], w13_hi[:, 1, e, hid], w13_lo[:, 1, e, hid], h2_hi[:, b % 2], h2_lo[:, b % 2]).then_inc(h3_ps, 1)

                if g >= DOWN and (g - DOWN) % KB == 0 and (ex := (g - DOWN) // KB) < NB * NE:
                    pe.wait_ge(hs_ready, KB * ex + KB)
                    if ex == 0:
                        pe.wait_ge(w2f_ready, U // FUSED)
                        take("Y")
                    else:
                        pe.wait_ge(yg_ready, ex)
                    for c in range(C):
                        for k in range(KB):
                            mm = nc.tensor.matmul(tile(Y, c), tile(hs[:, (KB * ex + k) % 4], c), w2f[:, (ex % NE) * KB + k, :],
                                                  start=(k == 0), stop=(k == KB - 1))
                    mm.then_inc(y_ps, 1)

        @block.vector
        def _(dve):
            def over(ap):
                return ap.unsqueeze(2).to_broadcast([P, C, NE])

            def token_stats(src, b, which):
                chain, st, mo = ln_chain[which], stats[:, b % 2, which], mv[:, b % 2, which]
                for c in range(C):
                    nc.vector.bn_stats(st[:, c, :], src[:, c, :]).then_inc(chain, 1)
                for c in range(C):
                    dve.wait_ge(chain, LNC * b + c + 1)
                    nc.vector.bn_aggr(mo[:, c, :], st[:, c, :]).then_inc(chain, 1)

            def normalise(src, b, which):
                chain, mo, r = ln_chain[which], mv[:, b % 2, which], rstd[:, b % 2, which]
                dve.wait_ge(sd_ready[which], b + 1)
                nc.vector.reciprocal(r, sd[:, b % 2, which]).then_inc(chain, 1)
                dve.wait_ge(chain, LNC * (b + 1))
                for c in range(C):
                    nc.vector.tensor_scalar(xn[:, which, c, :], src[:, c, :], mo[:, c, 0:1], r[:, c:c + 1],
                                            ALU.subtract, ALU.mult).then_inc(xn_ready[which], 1)

            nc.vector.memset(eps[:], EPS).then_inc(eps_set, 1)
            for g in SLOTS:
                if 1 <= g < NB * U + 1:
                    n = g - 1
                    if n == 0:
                        dve.wait_ge(small_in, SMALL)
                    dve.wait_ge(h3_ps, n + 1)
                    dve.wait_ge(h1b_ready, n + 1)
                    if n >= 2:
                        dve.wait_ge(hs_ready, n - 1)
                    nc.vector.scalar_tensor_tensor(hu[:, n % 2], H3[n % 2], b13[:, 1, n % U:n % U + 1], h1b[:, n % 2],
                                                   ALU.add, ALU.mult).then_inc(hu_ready, 1)
                if g > DOWN and (g - DOWN - 1) % KB == 0 and (ex := (g - DOWN - 1) // KB) < NB * NE:
                    b, e = divmod(ex, NE)
                    dve.wait_ge(y_ps, ex + 1)
                    if e == 0:
                        dve.wait_ge(gw_ready, b + 1)
                    if ex >= 2:
                        dve.wait_ge(acc_step, ex - 1)
                    nc.vector.tensor_tensor(yg[:, ex % 2], tiled(Y), gw[:, b % 2, :, e:e + 1].to_broadcast([P, C, D]), ALU.mult).then_inc(yg_ready, 1)

                if g == NB * U + DOWN - 1:
                    dve.wait_ge(yg_ready, NB * NE)
                    dve.wait_ge(acc_step, NB * NE - 1)
                    nc.vector.tensor_tensor(acc[:, (NB - 1) % 2], acc[:, (NB - 1) % 2], yg[:, (NB * NE - 1) % 2], ALU.add).then_inc(acc_step, 1)
                if (b := closing(g, SUM)) is not None:
                    dve.wait_ge(acc_step, NE * (b + 1))
                    dve.wait_ge(x2f_ready, b + 1)
                    for part in row_parts(b):
                        n = part.stop - part.start
                        nc.vector.tensor_tensor(ffg[:, part], acc[:, b % 2, part], gmod[:, GB, b:b + 1, :].to_broadcast([P, n, D]), ALU.mult).then_inc(ffg_ready, 1)
                        dve.wait_ge(ffg_ready, parts_before(b, part) + 1)
                        nc.vector.tensor_tensor(x2f[:, b % 2, part], ffg[:, part], x2f[:, b % 2, part], ALU.add).then_inc(res_ready, 1)

                if (b := at(g, HT)) is not None:
                    if b == 0:
                        dve.wait_ge(mod_ready, 2)
                    dve.wait_ge(xt_ps, b + 1)
                    nc.vector.tensor_scalar(h_t[:], M, mod[:, CA, b:b + 1], mod[:, SA, b:b + 1], ALU.mult, ALU.add).then_inc(h_ready, 1)
                    dve.wait_ge(h_ready, b + 1)
                    if b >= 2:
                        dve.wait_ge(v_ps, DH * (b - 1))
                    nc.vector.tensor_copy(h_hi[:, b % 2], h_t[:]).then_inc(h_hi_ready, 1)
                    dve.wait_ge(h_hi_ready, b + 1)
                    nc.vector.tensor_tensor(h_lo[:, b % 2], h_t[:], h_hi[:, b % 2].bitcast(F32), ALU.subtract).then_inc(h_lo_ready, 1)
                for step, names, done, read, used, part in ((PK, K_BANKS, k_ps, rope_k, khat_ready, 0), (PQ, Q_BANKS, q_ps, rope_q, qhat_ready, 2)):
                    if (b := at(g, step)) is not None:
                        if b == 0:
                            dve.wait_ge(cst_in, 16)
                        if b >= 1:
                            dve.wait_ge(used, b)
                        for i, tab in enumerate((cos, sin)):
                            dve.wait_ge(done, 2 * b + i + 1)
                            nc.vector.tensor_tensor(rope[:, part + i], BANK[names[b >= AHEAD][i]], tab, ALU.mult).then_inc(read, 1)
                if at(g, DV0 + DH) == 0:
                    dve.wait_ge(small_in, SMALL)
                    nc.vector.tensor_scalar(gn_scale[:], gn_sb[:, 0:1], SCALING, None, ALU.mult).then_inc(gn_ready, 1)
                for e in range(ON_VECTOR):
                    if g == SPLIT_LO[e]:
                        dve.wait_ge(w13_hi_ready, e + 1)
                        nc.vector.tensor_tensor(w13_lo[:, :, e], w13[:, :, e], w13_hi[:, :, e].bitcast(F32), ALU.subtract).then_inc(w13_lo_ready, 1)
                if (b := at(g, RST)) is not None:
                    dve.wait_ge(grst_ps, b + 1)
                    dve.wait_ge(osb_ready, b + 1)
                    nc.vector.tensor_tensor(z1[:], M, o_sb[:], ALU.mult).then_inc(z1_ready, 1)
                    dve.wait_ge(z1_ready, b + 1)
                    dve.wait_ge(gate_ready, b + 1)
                    if b >= 1:
                        dve.wait_ge(wo_ps, b)
                    nc.vector.scalar_tensor_tensor(z3[:], z1[:], gn_sb[:, 1:2], gate[:, b % 2], ALU.add, ALU.mult).then_inc(z3_ready, 1)
                if (b := at(g, WO)) is not None:
                    dve.wait_ge(wo_ps, b + 1)
                    dve.wait_ge(gmod_ready, 2)
                    nc.vector.tensor_tensor(att[:], tiled(M), gmod[:, GA, b:b + 1, :].to_broadcast([P, C, D]), ALU.mult).then_inc(att_ready, 1)
                    dve.wait_ge(att_ready, b + 1)
                    if b >= 2:
                        dve.wait_ge(x2f_ready, b - 1)
                    nc.vector.tensor_tensor(x2[:, b % 2], att[:], xs[:, b], ALU.add).then_inc(x2_ready, 1)
                    if b == 0:
                        dve.wait_ge(x2_ready, b + 1)
                        token_stats(x2[:, b % 2], b, 1)
                if (b := at(g, LN2)) is not None:
                    dve.wait_ge(x2t_ps, b + 1)
                    if b >= 1:
                        dve.wait_ge(lg_ps, b)
                    nc.vector.tensor_scalar(h2_t[:], M, mod[:, CB, b:b + 1], mod[:, SB, b:b + 1], ALU.mult, ALU.add).then_inc(h2_ready, 1)
                    dve.wait_ge(h2_ready, b + 1)
                    if b >= 2:
                        dve.wait_ge(h3_ps, U * (b - 1))
                    nc.vector.tensor_copy(h2_hi[:, b % 2], h2_t[:]).then_inc(h2_hi_ready, 1)
                    dve.wait_ge(h2_hi_ready, b + 1)
                    nc.vector.tensor_tensor(h2_lo[:, b % 2], h2_t[:], h2_hi[:, b % 2].bitcast(F32), ALU.subtract).then_inc(h2_lo_ready, 1)
                if (b := at(g, LOG)) is not None:
                    k = LG * b
                    dve.wait_ge(lg_ps, b + 1)
                    nc.vector.tensor_tensor(lg[:, 0], M[:, 0:C * NE].rearrange("p (c e) -> p c e", c=C),
                                            bg_bc[:].unsqueeze(1).to_broadcast([P, C, NE]), ALU.add).then_inc(lg_steps, 1)
                    dve.wait_ge(lg_steps, k + 1)
                    nc.vector.tensor_reduce(lmax[:], lg[:, 0], AX.X, ALU.max).then_inc(lg_steps, 1)
                    dve.wait_ge(lg_steps, k + 2)
                    nc.vector.tensor_tensor(lg[:, 1], lg[:, 0], over(lmax[:]), ALU.subtract).then_inc(lg_steps, 1)
                if (b := at(g, B2)) is not None:
                    dve.wait_ge(b2_ps, b + 1)
                    if b == 0:
                        dve.wait_ge(w2f_ps, U // FUSED)
                    if b >= 2:
                        dve.wait_ge(ffg_ready, b - 1)
                    nc.vector.tensor_copy(acc[:, b % 2], tiled(M)).then_inc(acc_set, 1)
                if (b := at(g, NRM2)) is not None:
                    if b >= 1:
                        dve.wait_ge(x2t_ps, b)
                    normalise(x2[:, b % 2], b, 1)
                if (b := at(g, RSD)) is not None:
                    dve.wait_ge(gsd_ready, b + 1)
                    nc.vector.reciprocal(grs[:], gsd[:]).then_inc(grs_ready, 1)
                    dve.wait_ge(grs_ready, b + 1)
                    if b >= 1:
                        dve.wait_ge(grst_ps, b)
                    nc.vector.tensor_copy(grs_bc[:].rearrange("p c (h d) -> p (c h) d", d=DH),
                                          grs[:].unsqueeze(2).to_broadcast([P, C * H, DH])).then_inc(grsbc_ready, 1)

                for v in range(DH):
                    if (b := at(g, DV0 + v)) is not None:
                        n = DH * b + v
                        dve.wait_ge(v_ps, n + 1)
                        if v == 0:
                            dve.wait_ge(khat_ready, b + 1)
                        if n >= 2:
                            dve.wait_ge(state_ready, n - 1)
                        nc.vector.tensor_tensor(kv[:, n % 2], BANK[v_bank(b, v)], khat[:, b % 2], ALU.mult).then_inc(kv_ready, 1)
                        dve.wait_ge(kv_ready, n + 1)
                        if n >= 3:
                            dve.wait_ge(qs_ready, n - 2)
                        nc.vector.tensor_tensor_scan(state[:, n % 3], gamma.to_broadcast([P, S]), kv[:, n % 2], 0.0,
                                                     ALU.mult, ALU.add).then_inc(state_ready, 1)

                if (b := at(g, WO)) is not None and b > 0:
                    dve.wait_ge(x2_ready, b + 1)
                    token_stats(x2[:, b % 2], b, 1)
                if (b := at(g, LN1)) is not None:
                    dve.wait_ge(x_in[b], 16)
                    token_stats(xs[:, b], b, 0)
                if (b := at(g, NRM1)) is not None:
                    if b >= 1:
                        dve.wait_ge(xt_ps, b)
                    normalise(xs[:, b], b, 0)
                    if b == 0:
                        dve.wait_ge(wat_hi_ready, 1)
                        nc.vector.tensor_tensor(wat_lo[:], wat[:], wat_hi[:].bitcast(F32), ALU.subtract).then_inc(wat_lo_ready, 1)
                        dve.wait_ge(mod_ps, 1)
                        m_ps = Y[:, 0:6 * NB].rearrange("p (i b) -> p i b", i=6)
                        nc.vector.tensor_scalar(mod[:, 0::2], m_ps[:, 0:4:2], 0.0, None, ALU.add).then_inc(mod_ready, 1)
                        nc.vector.tensor_scalar(mod[:, 1::2], m_ps[:, 1:4:2], 1.0, None, ALU.add).then_inc(mod_ready, 1)
                        nc.vector.tensor_scalar(gcol[:, 0], m_ps[:, 4:6], 0.0, None, ALU.add).then_inc(mod_ready, 1)
                        dve.wait_ge(mod_ready, 3)
                        nc.vector.tensor_scalar(gcol[:, 1], gcol[:, 0], 0.0, 2.0, ALU.is_ge, ALU.mult).then_inc(gcol_steps, 1)
                        dve.wait_ge(gcol_steps, 1)
                        nc.vector.tensor_scalar(gcol[:, 2], gcol[:, 1], -1.0, None, ALU.add).then_inc(gcol_steps, 1)
                        dve.wait_ge(gcol_steps, 2)
                        nc.vector.tensor_tensor(gcol[:, 3], gcol[:, 2], gcol[:, 0], ALU.mult).then_inc(gcol_steps, 1)
                        dve.wait_ge(gcol_steps, 3)
                        nc.vector.scalar_tensor_tensor(gcol[:, 4], gcol[:, 3], 0.25, gcol[:, 2], ALU.max, ALU.mult).then_inc(gcol_steps, 1)
                if (b := at(g, TOP)) is not None:
                    k = LG * b
                    dve.wait_ge(exp_ready, b + 1)
                    nc.vector.tensor_reduce(lsum[:], lg[:, 2], AX.X, ALU.add).then_inc(lg_steps, 1)
                    dve.wait_ge(lg_steps, k + 4)
                    nc.vector.reciprocal(lrec[:], lsum[:]).then_inc(lg_steps, 1)
                    dve.wait_ge(lg_steps, k + 5)
                    nc.vector.tensor_tensor(prob[:, b % 2], lg[:, 2], over(lrec[:]), ALU.mult).then_inc(lg_steps, 1)
                    dve.wait_ge(lg_steps, k + 6)
                    if b >= 1:
                        dve.wait_ge(ahead_ready, 2 * b)
                    nc.vector.tensor_tensor(cmp[:, 0], *each_pair(b), ALU.is_equal).then_inc(lg_steps, 1)
                    nc.vector.tensor_tensor(cmp[:, 1], *each_pair(b), ALU.is_gt).then_inc(lg_steps, 1)
                if (b := at(g, RANK)) is not None:
                    k = LG * b
                    dve.wait_ge(ahead_ready, 2 * b + 2)
                    nc.vector.tensor_reduce(rank[:], cmp[:, 3], AX.X, ALU.add).then_inc(lg_steps, 1)
                    dve.wait_ge(lg_steps, k + 9)
                    if b >= 2:
                        dve.wait_ge(yg_ready, NE * (b - 1))
                    nc.vector.scalar_tensor_tensor(gw[:, b % 2], rank[:], float(TOPK), prob[:, b % 2], ALU.is_lt, ALU.mult).then_inc(gw_ready, 1)

        @block.scalar
        def _(act):
            act.dma_start(ct_sb[:], c_t).then_inc(ct_in, 16)
            act.dma_start(wmod_sb[:], wmod.rearrange("p (j d) -> p j d", d=D)).then_inc(mod_in, 16)
            act.wait_ge(ct_in, 16)
            nc.scalar.activation(sct[:], ct_sb[:], ACT.Silu).then_inc(sct_ready, 1)

            def deviation(b, which):
                act.wait_ge(ln_chain[which], LNC * b + 2 * C)
                nc.scalar.activation(sd[:, b % 2, which], mv[:, b % 2, which, :, 1], ACT.Sqrt, bias=eps[:]).then_inc(sd_ready[which], 1)

            for g in SLOTS:
                if (b := at(g, NRM1)) is not None:
                    if b == 0:
                        act.wait_ge(eps_set, 1)
                    deviation(b, 0)
                if at(g, NRM2) == 0:
                    deviation(0, 1)
                if (b := at(g, TOP)) is not None:
                    act.wait_ge(lg_steps, LG * b + 3)
                    nc.scalar.activation(lg[:, 2], lg[:, 1], ACT.Exp).then_inc(exp_ready, 1)

                for v in range(2, DH + 2):
                    if (b := at(g, DV0 + v)) is not None and b >= AHEAD:
                        n = DH * b + v - 2
                        act.wait_ge(qs_ready, n + 1)
                        if n >= DH * AHEAD + 2:
                            act.wait_ge(o_step, n - 1)
                        nc.scalar.activation(qs_hi[:, n % 2], qs[:, n % 3], ACT.Copy).then_inc(qs_hi_ready, 1)

                if 1 <= g < NB * U + 1:
                    n = g - 1
                    if n == 0:
                        act.wait_ge(small_in, SMALL)
                    act.wait_ge(h1_ps, n + 1)
                    if n >= 2:
                        act.wait_ge(hu_ready, n - 1)
                    nc.scalar.activation(h1b[:, n % 2], H1[n % 2], ACT.Identity, bias=b13[:, 0, n % U:n % U + 1]).then_inc(h1b_ready, 1)
                if 2 <= g < NB * U + 2:
                    n = g - 2
                    act.wait_ge(hu_ready, n + 1)
                    if n >= 4:
                        act.wait_ge(y_ps, (n - 4) // KB + 1)
                    nc.scalar.activation(hs[:, n % 4], hu[:, n % 2], ACT.Silu).then_inc(hs_ready, 1)

                if (b := at(g, NRM2)) is not None and b > 0:
                    deviation(b, 1)

                if g == FRONT[0] + NRM1:
                    act.wait_ge(wat_in, 16)
                    nc.scalar.activation(wat_hi[:], wat[:], ACT.Copy).then_inc(wat_hi_ready, 1)
                    act.wait_ge(wat_hi_ready, 1)
                    nc.scalar.activation(wv_hi[:].rearrange("p v h k -> p h v k"), by_head(wat_hi), ACT.Copy).then_inc(wv_ready, 1)
                if g == FRONT[0] + HT:
                    act.wait_ge(gcol_steps, 4)
                    nc.scalar.activation(g_rep[:], gcol[:, 4].unsqueeze(3).to_broadcast([P, 2, NB, P]), ACT.Copy).then_inc(grep_ready, 1)
                for step, j, bank in ((PK, GA, O), (DV0 + 1, GB, M)):
                    if at(g, step) == 0:
                        act.wait_ge(gmod_ps, j + 1)
                        nc.scalar.activation(gmod[:, j], tiled(bank), ACT.Copy).then_inc(gmod_ready, 1)
                if (b := at(g, PG)) is not None:
                    act.wait_ge(g_ps, b + 1)
                    if b >= 2:
                        act.wait_ge(z3_ready, b - 1)
                    nc.scalar.activation(gate[:, b % 2], V, ACT.Silu).then_inc(gate_ready, 1)
                if at(g, PQ) == 0:
                    act.wait_ge(gather_in, 16)
                    nc.scalar.activation(gather[:].rearrange("p v d -> p (v d)"), gather_stage, ACT.Copy).then_inc(gather_ready, 1)
                if g == SPLIT_HI:
                    act.wait_ge(w13_in, 32)
                    for e in range(NE):
                        nc.scalar.activation(w13_hi[:, :, e], w13[:, :, e], ACT.Copy).then_inc(w13_hi_ready, 1)
                if (b := at(g, SQ)) is not None:
                    if b == 0:
                        act.wait_ge(gn_ready, 1)
                    act.wait_ge(o_step, DH * (b + 1))
                    if b >= 1:
                        act.wait_ge(z1_ready, b)
                        act.wait_ge(var_ps, b)
                    nc.scalar.activation(o_sq[:], O, ACT.Square, scale=SCALING).then_inc(osq_ready, 1)
                    nc.scalar.activation(o_sb[:], O, ACT.Copy, scale=gn_scale[:]).then_inc(osb_ready, 1)
                if (b := at(g, VAR)) is not None:
                    act.wait_ge(var_ps, b + 1)
                    if b >= 1:
                        act.wait_ge(grs_ready, b)
                    nc.scalar.activation(gsd[:], M[:, 0:C * H], ACT.Sqrt, bias=eps[:]).then_inc(gsd_ready, 1)
                if (b := at(g, GWT)) is not None:
                    act.wait_ge(gwt_ps, b + 1)
                    if b >= 1:
                        act.wait_ge(b2_ps, b)
                    nc.scalar.activation(gw_t[0:NE], M[0:NE], ACT.Copy).then_inc(gwt_ready, 1)
                if (n := g - FUSE) in range(U // FUSED):
                    act.wait_ge(w2f_ps, n + 1)
                    bank = (H1[0], H3[0], H1[1], H3[1])[n]
                    nc.scalar.activation(w2f[:, n * FUSED:(n + 1) * FUSED], tiled(bank), ACT.Copy).then_inc(w2f_ready, 1)
                    if n == 0:
                        act.wait_ge(b2f_ps, 1)
                        nc.scalar.activation(b2f[0:NE], M[0:NE, 0:D], ACT.Copy).then_inc(b2f_ready, 1)

        @block.gpsimd
        def _(pool):
            for g in SLOTS:
                if (b := at(g, PK)) is not None:
                    pool.wait_ge(rope_k, 2 * b + 2)
                    if b >= 2:
                        pool.wait_ge(kv_ready, DH * (b - 1))
                    nc.gpsimd.tensor_tensor(khat[:, b % 2], rope[:, 0], rope[:, 1], ALU.add).then_inc(khat_ready, 1)
                if g == FRONT[0] + PK:
                    pool.wait_ge(wat_lo_ready, 1)
                    nc.gpsimd.tensor_scalar(wv_lo[:].rearrange("p v h k -> p h v k"), by_head(wat_lo), 1.0, 0.0, ALU.mult, ALU.add).then_inc(wv_ready, 1)
                if (b := at(g, PQ)) is not None:
                    pool.wait_ge(rope_q, 2 * b + 2)
                    nc.gpsimd.tensor_tensor(qhat[:, b % 2], rope[:, 2], rope[:, 3], ALU.add).then_inc(qhat_ready, 1)
                for v in range(1, DH + 1):
                    if (b := at(g, DV0 + v)) is not None:
                        n = DH * b + v - 1
                        pool.wait_ge(state_ready, n + 1)
                        if v == 1:
                            pool.wait_ge(qhat_ready, b + 1)
                        if n - 3 >= DH * AHEAD:
                            pool.wait_ge(qs_lo_ready, n - 2 - DH * AHEAD)
                        elif n >= 3:
                            pool.wait_ge(o_step, n - 2)
                        nc.gpsimd.tensor_tensor(qs[:, n % 3], state[:, n % 3], qhat[:, b % 2], ALU.mult).then_inc(qs_ready, 1)
                for v in range(2, DH + 2):
                    if (b := at(g, DV0 + v)) is not None and b >= AHEAD:
                        n = DH * b + v - 2
                        pool.wait_ge(qs_hi_ready, n - DH * AHEAD + 1)
                        if n >= DH * AHEAD + 2:
                            pool.wait_ge(o_step, n - 1)
                        nc.gpsimd.tensor_tensor(qs_lo[:, n % 2], qs[:, n % 3], qs_hi[:, n % 2].bitcast(F32), ALU.subtract).then_inc(qs_lo_ready, 1)
                for e in range(ON_VECTOR, NE):
                    if g == SPLIT_LO[e]:
                        pool.wait_ge(w13_hi_ready, e + 1)
                        nc.gpsimd.tensor_tensor(w13_lo[:, :, e], w13[:, :, e], w13_hi[:, :, e].bitcast(F32), ALU.subtract).then_inc(w13_lo_ready, 1)
                if (b := at(g, NRM2)) is not None:
                    if b == 0:
                        pool.wait_ge(small_in, SMALL)
                        pool.wait_ge(gmod_ready, 2)
                        nc.gpsimd.tensor_tensor(gb_bf[:], gmod[:, GB], bf_bc[:].unsqueeze(1).to_broadcast([P, NB, D]), ALU.mult).then_inc(gbbf_ready, 1)
                        pool.wait_ge(gbbf_ready, 1)
                    pool.wait_ge(x2_ready, b + 1)
                    if b >= 2:
                        pool.wait_ge(stored, 16 * (b - 1))
                    nc.gpsimd.tensor_tensor(x2f[:, b % 2], x2[:, b % 2], gb_bf[:, b:b + 1, :].to_broadcast([P, C, D]), ALU.add).then_inc(x2f_ready, 1)
                if (b := at(g, TOP)) is not None:
                    pool.wait_ge(lg_steps, LG * b + 7)
                    if b >= 1:
                        pool.wait_ge(lg_steps, LG * b)
                    nc.gpsimd.tensor_tensor(cmp[:, 2], cmp[:, 0], later.unsqueeze(1).to_broadcast([P, C, NE, NE]), ALU.mult).then_inc(ahead_ready, 1)
                    pool.wait_ge(ahead_ready, 2 * b + 1)
                    pool.wait_ge(lg_steps, LG * b + 8)
                    nc.gpsimd.tensor_tensor(cmp[:, 3], cmp[:, 2], cmp[:, 1], ALU.add).then_inc(ahead_ready, 1)
                if g > DOWN and (g - DOWN - 1) % KB == 0 and (ex := (g - DOWN - 1) // KB) < NB * NE - 1:
                    b = ex // NE
                    pool.wait_ge(yg_ready, ex + 1)
                    if ex % NE == 0:
                        pool.wait_ge(acc_set, b + 1)
                    else:
                        pool.wait_ge(acc_step, ex)
                    nc.gpsimd.tensor_tensor(acc[:, b % 2], acc[:, b % 2], yg[:, ex % 2], ALU.add).then_inc(acc_step, 1)


def kernel(**inputs):
    import concourse.bacc as bacc
    from concourse.bass_utils import run_bass_kernel_spmd

    a = {k.replace("L0_", ""): np.asarray(v) for k, v in inputs.items()}

    def turned(w):
        return w.reshape(D, H, 2, DH // 2)[:, :, ::-1].reshape(D, D)

    wq, wk = a["attn_Wq"].T, a["attn_Wk"].T
    arrays = {
        "x": a["attn_x"],
        "w_att": np.stack([wk, turned(wk), wq, turned(wq), a["attn_Wg"].T, a["attn_Wv"].T], axis=1),
        "wo_t": a["attn_Wo"].T,
        "gn": np.stack([a["attn_gn_w"], a["attn_gn_b"]], axis=1),
        "w1": a["ffn_W1"], "b1_t": a["ffn_b1"].reshape(U, P).T,
        "w3": a["ffn_W3"], "b3_t": a["ffn_b3"].reshape(U, P).T,
        "w2_t": a["ffn_W2"].transpose(2, 0, 1).reshape(D, U, P), "b2_t": a["ffn_b2"].T,
        "wg": a["ffn_Wg"], "bg": a["ffn_bg"].reshape(1, NE),
        "wf": a["ffn_Wf"], "bf": a["ffn_bf"].reshape(1, D),
        "c_t": a["c"].T, "wmod": a["wmod"],
        "consts": shape_constants(),
    }
    arrays = {k: np.ascontiguousarray(v) for k, v in arrays.items()}
    nc = bacc.Bacc("TRN2", target_bir_lowering=False, num_devices=1)
    args = [nc.dram_tensor(k, v.shape, mybir.dt.from_np(v.dtype), kind="ExternalInput").ap() for k, v in arrays.items()]
    args.append(nc.dram_tensor("out", (NB, S, D), F32, kind="ExternalOutput").ap())
    build(nc, *args)
    r = run_bass_kernel_spmd(nc, [arrays], core_ids=[0])
    return r.results[0]["out"]
```
